# Optimizing a Trainium2 kernel written in Bass

```python
import numpy as np
import jax
import jax.numpy as jnp

def _softmax(x, axis=-1):
    return jax.nn.softmax(x, axis=axis)

def _gelu(x):
    return jax.nn.gelu(x, approximate=True)

def _silu(x):
    return jax.nn.silu(x)

def _sigmoid(x):
    return jax.nn.sigmoid(x)

def _layernorm(x, axis=-1, eps=1e-05):
    m = jnp.mean(x, axis=axis, keepdims=True)
    v = jnp.var(x, axis=axis, keepdims=True)
    return (x - m) / jnp.sqrt(v + eps)

def _scatter_add(tgt, idx, src, axis=0):
    return tgt.at[idx].add(src)

def _segment_sum(src, seg, n):
    return jax.ops.segment_sum(src, seg, n)
kernel_name = 'mk_vit_tower_d1_tok_img768_r4_41cbb2'

def setup_inputs(seed: int=0):
    np.random.seed(seed)
    _w = jnp.asarray

    def _rec_inputs():
        import jax
        import jax.numpy as jnp
        _rk = jax.random.key(seed)
        x = -0.000356955 + 1 * jax.random.normal(jax.random.fold_in(_rk, 1), (64, 3, 224, 224), jnp.float32)
        return x
    x = _rec_inputs()

    def _L0_tok_setup():
        import jax, jax.numpy as jnp
        import numpy as np
        C, H, W_IMG = (3, 224, 224)
        NP = 14
        PS = H // NP
        D_IN = C * PS * PS
        D = 192
        SEQ = NP * NP + 1
        B = 128

        def _sinusoidal_pos_embed(seq_len, d):
            i = np.arange(seq_len, dtype=np.float64)[:, None]
            j = np.arange(d, dtype=np.float64)[None, :]
            angle = i / np.power(10000.0, (j - j % 2) / d)
            pe = np.where(j % 2 == 0, np.sin(angle), np.cos(angle))
            return jnp.asarray(pe, dtype=jnp.float32)
        key = jax.random.key(seed)
        kx, kw, kc = jax.random.split(key, 3)
        x = jax.random.normal(kx, (B, C, H, W_IMG), dtype=jnp.float32)
        W = jax.random.normal(kw, (D, D_IN), dtype=jnp.float32) * 0.02
        b = jnp.zeros((D,), dtype=jnp.float32)
        class_token = jax.random.uniform(kc, (1, D), dtype=jnp.float32)
        pos_embed = _sinusoidal_pos_embed(SEQ, D)
        return {'x': x, 'W': W, 'b': b, 'class_token': class_token, 'pos_embed': pos_embed}
    _L0_tok_all = _L0_tok_setup()
    _L0_tok_in = {k: v for k, v in _L0_tok_all.items() if k in ('W', 'b', 'class_token', 'pos_embed')}
    del _L0_tok_all

    def _L0_attn_setup():
        import jax, jax.numpy as jnp
        import numpy as np
        import math
        DIM = 192
        NUM_HEADS = 12
        HEAD_DIM = DIM // NUM_HEADS
        ORDER = 2
        SCALE = HEAD_DIM ** (-0.5)
        key = jax.random.key(seed)
        ks = jax.random.split(key, 5)
        B, N, C = (8, 256, DIM)
        x = jax.random.normal(ks[0], (B, N, C), dtype=jnp.float32)
        w_qkv = jax.random.normal(ks[1], (C, 3 * C), dtype=jnp.float32) * C ** (-0.5)
        w_proj = jax.random.normal(ks[2], (C, C), dtype=jnp.float32) * C ** (-0.5)
        b_proj = jax.random.normal(ks[3], (C,), dtype=jnp.float32) * 0.02
        return {'x': x, 'w_qkv': w_qkv, 'w_proj': w_proj, 'b_proj': b_proj}
    _L0_attn_all = _L0_attn_setup()
    _L0_attn_in = {k: v for k, v in _L0_attn_all.items() if k in ('w_qkv', 'w_proj', 'b_proj')}
    del _L0_attn_all

    def _L0_ffn_setup():
        import jax, jax.numpy as jnp
        import numpy as np
        H = 12
        ALPHA = (1, 2, 3)
        DEPTH = 5
        BLOCK_DEPTH = 3
        TOTAL_DEPTH_M1 = 14 - 1
        SMALL_ACTIVE = BLOCK_DEPTH <= DEPTH <= TOTAL_DEPTH_M1 - BLOCK_DEPTH

        def _ln(x, g, b, eps=1e-05):
            m = jnp.mean(x, axis=-1, keepdims=True)
            v = jnp.mean((x - m) ** 2, axis=-1, keepdims=True)
            return (x - m) * jax.lax.rsqrt(v + eps) * g + b

        def _attn_branch(xp, w_qkv, w_proj, b_proj, keep_heads, keep_ch):
            B2, N, C = xp.shape
            hd = C // H
            scale = hd ** (-0.5)
            qkv = (xp @ w_qkv).reshape(B2, N, 3, H, hd).transpose(2, 0, 3, 1, 4)
            hmask = (jnp.arange(H) < keep_heads).astype(xp.dtype)[None, :, None, None]
            q, k, v = (qkv[0] * hmask, qkv[1] * hmask, qkv[2] * hmask)
            a = jax.nn.softmax(jnp.einsum('bhnd,bhmd->bhnm', q, k) * scale, axis=-1)
            o = jnp.einsum('bhnm,bhmd->bhnd', a, v).transpose(0, 2, 1, 3).reshape(B2, N, C)
            o = o @ w_proj + b_proj
            cmask = (jnp.arange(C) < keep_ch).astype(xp.dtype)
            return o * cmask

        def _mlp_branch(xp, w1, b1, w2, b2, keep_ch):
            C = xp.shape[-1]
            cmask = (jnp.arange(C) < keep_ch).astype(xp.dtype)
            h = jax.nn.gelu(xp * cmask @ w1 + b1, approximate=False)
            return (h @ w2 + b2) * cmask
        key = jax.random.key(seed)
        ks = jax.random.split(key, 8)
        B, N, C = (64, 257, 192)
        HID = 4 * C

        def w(k, shape):
            return jax.random.normal(k, shape, jnp.float32) * 0.02
        return {'x': jax.random.normal(ks[0], (B, N, C), jnp.float32), 'gumbel_weights': jax.random.uniform(ks[1], (3,), jnp.float32), 'n1l_g': jnp.ones((C,), jnp.float32), 'n1l_b': jnp.zeros((C,), jnp.float32), 'n1s_g': jnp.ones((C,), jnp.float32), 'n1s_b': jnp.zeros((C,), jnp.float32), 'w_qkv': w(ks[2], (C, 3 * C)), 'w_proj': w(ks[3], (C, C)), 'b_proj': jnp.zeros((C,), jnp.float32), 'n2l_g': jnp.ones((C,), jnp.float32), 'n2l_b': jnp.zeros((C,), jnp.float32), 'n2s_g': jnp.ones((C,), jnp.float32), 'n2s_b': jnp.zeros((C,), jnp.float32), 'w_fc1': w(ks[4], (C, HID)), 'b_fc1': jnp.zeros((HID,), jnp.float32), 'w_fc2': w(ks[5], (HID, C)), 'b_fc2': jnp.zeros((C,), jnp.float32)}
    _L0_ffn_all = _L0_ffn_setup()
    _L0_ffn_in = {k: v for k, v in _L0_ffn_all.items() if k in ('gumbel_weights', 'n1l_g', 'n1l_b', 'n1s_g', 'n1s_b', 'w_qkv', 'w_proj', 'b_proj', 'n2l_g', 'n2l_b', 'n2s_g', 'n2s_b', 'w_fc1', 'b_fc1', 'w_fc2', 'b_fc2')}
    del _L0_ffn_all
    return {'x': x, 'L0_tok_W': _L0_tok_in['W'], 'L0_tok_b': _L0_tok_in['b'], 'L0_tok_class_token': _L0_tok_in['class_token'], 'L0_tok_pos_embed': _L0_tok_in['pos_embed'], 'L0_attn_w_qkv': _L0_attn_in['w_qkv'], 'L0_attn_w_proj': _L0_attn_in['w_proj'], 'L0_attn_b_proj': _L0_attn_in['b_proj'], 'L0_ffn_gumbel_weights': _L0_ffn_in['gumbel_weights'], 'L0_ffn_n1l_g': _L0_ffn_in['n1l_g'], 'L0_ffn_n1l_b': _L0_ffn_in['n1l_b'], 'L0_ffn_n1s_g': _L0_ffn_in['n1s_g'], 'L0_ffn_n1s_b': _L0_ffn_in['n1s_b'], 'L0_ffn_w_qkv': _L0_ffn_in['w_qkv'], 'L0_ffn_w_proj': _L0_ffn_in['w_proj'], 'L0_ffn_b_proj': _L0_ffn_in['b_proj'], 'L0_ffn_n2l_g': _L0_ffn_in['n2l_g'], 'L0_ffn_n2l_b': _L0_ffn_in['n2l_b'], 'L0_ffn_n2s_g': _L0_ffn_in['n2s_g'], 'L0_ffn_n2s_b': _L0_ffn_in['n2s_b'], 'L0_ffn_w_fc1': _L0_ffn_in['w_fc1'], 'L0_ffn_b_fc1': _L0_ffn_in['b_fc1'], 'L0_ffn_w_fc2': _L0_ffn_in['w_fc2'], 'L0_ffn_b_fc2': _L0_ffn_in['b_fc2']}

def reference(x, L0_tok_W, L0_tok_b, L0_tok_class_token, L0_tok_pos_embed, L0_attn_w_qkv, L0_attn_w_proj, L0_attn_b_proj, L0_ffn_gumbel_weights, L0_ffn_n1l_g, L0_ffn_n1l_b, L0_ffn_n1s_g, L0_ffn_n1s_b, L0_ffn_w_qkv, L0_ffn_w_proj, L0_ffn_b_proj, L0_ffn_n2l_g, L0_ffn_n2l_b, L0_ffn_n2s_g, L0_ffn_n2s_b, L0_ffn_w_fc1, L0_ffn_b_fc1, L0_ffn_w_fc2, L0_ffn_b_fc2):
    import jax
    import jax.numpy as jnp

    def _L0_tok_ref(x, W, b, class_token, pos_embed):
        import jax, jax.numpy as jnp
        import numpy as np
        C, H, W_IMG = (3, 224, 224)
        NP = 14
        PS = H // NP
        D_IN = C * PS * PS
        D = 192
        SEQ = NP * NP + 1
        B = 128

        def _sinusoidal_pos_embed(seq_len, d):
            i = np.arange(seq_len, dtype=np.float64)[:, None]
            j = np.arange(d, dtype=np.float64)[None, :]
            angle = i / np.power(10000.0, (j - j % 2) / d)
            pe = np.where(j % 2 == 0, np.sin(angle), np.cos(angle))
            return jnp.asarray(pe, dtype=jnp.float32)
        n = x.shape[0]
        p = x.reshape(n, C, NP, PS, NP, PS)
        p = p.transpose(0, 2, 4, 1, 3, 5).reshape(n, NP * NP, D_IN)
        tokens = jnp.einsum('npd,hd->nph', p, W) + b
        cls = jnp.broadcast_to(class_token[None], (n, 1, D))
        tokens = jnp.concatenate([cls, tokens], axis=1)
        return tokens + pos_embed[None]

    def _L0_attn_ref(x, w_qkv, w_proj, b_proj):
        import jax, jax.numpy as jnp
        import numpy as np
        import math
        DIM = 192
        NUM_HEADS = 12
        HEAD_DIM = DIM // NUM_HEADS
        ORDER = 2
        SCALE = HEAD_DIM ** (-0.5)
        B, N, C = x.shape
        H, Dh = (NUM_HEADS, HEAD_DIM)
        qkv = (x @ w_qkv).reshape(B, N, 3, H, Dh)
        qkv = jnp.transpose(qkv, (2, 0, 3, 1, 4))
        q, k, v = (qkv[0], qkv[1], qkv[2])
        q = q * SCALE
        qk = jnp.einsum('bhnd,bhmd->bhnm', q, k)
        attn = jnp.ones_like(qk)
        x_power = qk
        for i in range(1, ORDER + 1):
            attn = attn + x_power / math.factorial(i)
            if i < ORDER:
                x_power = x_power * qk
        attn = jax.nn.relu(attn)
        attn = attn / jnp.sum(attn, axis=-1, keepdims=True)
        out = jnp.einsum('bhnm,bhmd->bhnd', attn, v)
        out = jnp.transpose(out, (0, 2, 1, 3)).reshape(B, N, C)
        return out @ w_proj + b_proj

    def _L0_ffn_ref(x, gumbel_weights, n1l_g, n1l_b, n1s_g, n1s_b, w_qkv, w_proj, b_proj, n2l_g, n2l_b, n2s_g, n2s_b, w_fc1, b_fc1, w_fc2, b_fc2):
        import jax, jax.numpy as jnp
        import numpy as np
        H = 12
        ALPHA = (1, 2, 3)
        DEPTH = 5
        BLOCK_DEPTH = 3
        TOTAL_DEPTH_M1 = 14 - 1
        SMALL_ACTIVE = BLOCK_DEPTH <= DEPTH <= TOTAL_DEPTH_M1 - BLOCK_DEPTH

        def _ln(x, g, b, eps=1e-05):
            m = jnp.mean(x, axis=-1, keepdims=True)
            v = jnp.mean((x - m) ** 2, axis=-1, keepdims=True)
            return (x - m) * jax.lax.rsqrt(v + eps) * g + b

        def _attn_branch(xp, w_qkv, w_proj, b_proj, keep_heads, keep_ch):
            B2, N, C = xp.shape
            hd = C // H
            scale = hd ** (-0.5)
            qkv = (xp @ w_qkv).reshape(B2, N, 3, H, hd).transpose(2, 0, 3, 1, 4)
            hmask = (jnp.arange(H) < keep_heads).astype(xp.dtype)[None, :, None, None]
            q, k, v = (qkv[0] * hmask, qkv[1] * hmask, qkv[2] * hmask)
            a = jax.nn.softmax(jnp.einsum('bhnd,bhmd->bhnm', q, k) * scale, axis=-1)
            o = jnp.einsum('bhnm,bhmd->bhnd', a, v).transpose(0, 2, 1, 3).reshape(B2, N, C)
            o = o @ w_proj + b_proj
            cmask = (jnp.arange(C) < keep_ch).astype(xp.dtype)
            return o * cmask

        def _mlp_branch(xp, w1, b1, w2, b2, keep_ch):
            C = xp.shape[-1]
            cmask = (jnp.arange(C) < keep_ch).astype(xp.dtype)
            h = jax.nn.gelu(xp * cmask @ w1 + b1, approximate=False)
            return (h @ w2 + b2) * cmask
        B, N, C = x.shape
        B2 = B // 2
        nl = _ln(x[:B2], n1l_g, n1l_b)
        ns = _ln(x[B2:], n1s_g, n1s_b)
        a_large = _attn_branch(nl, w_qkv, w_proj, b_proj, H, C)
        if SMALL_ACTIVE:
            a_small = sum((gumbel_weights[i] * _attn_branch(ns, w_qkv, w_proj, b_proj, H // ALPHA[i], C // ALPHA[i]) for i in range(3)))
            attn_out = jnp.concatenate([a_large, a_small], axis=0)
        else:
            attn_out = jnp.concatenate([a_large, a_large], axis=0)
        x = x + attn_out
        nl2 = _ln(x[:B2], n2l_g, n2l_b)
        ns2 = _ln(x[B2:], n2s_g, n2s_b)
        m_large = _mlp_branch(nl2, w_fc1, b_fc1, w_fc2, b_fc2, C)
        if SMALL_ACTIVE:
            m_small = sum((gumbel_weights[i] * _mlp_branch(ns2, w_fc1, b_fc1, w_fc2, b_fc2, C // ALPHA[i]) for i in range(3)))
            mlp_out = jnp.concatenate([m_large, m_small], axis=0)
        else:
            mlp_out = jnp.concatenate([m_large, m_large], axis=0)
        return x + mlp_out
    h = _L0_tok_ref(x, L0_tok_W, L0_tok_b, L0_tok_class_token, L0_tok_pos_embed)
    h = h + _L0_attn_ref(_layernorm(h, axis=-1), L0_attn_w_qkv, L0_attn_w_proj, L0_attn_b_proj)
    h = h + _L0_ffn_ref(_layernorm(h, axis=-1), L0_ffn_gumbel_weights, L0_ffn_n1l_g, L0_ffn_n1l_b, L0_ffn_n1s_g, L0_ffn_n1s_b, L0_ffn_w_qkv, L0_ffn_w_proj, L0_ffn_b_proj, L0_ffn_n2l_g, L0_ffn_n2l_b, L0_ffn_n2s_g, L0_ffn_n2s_b, L0_ffn_w_fc1, L0_ffn_b_fc1, L0_ffn_w_fc2, L0_ffn_b_fc2)
    return h

_drawn_inputs = setup_inputs


def setup_inputs(seed=0):
    import zlib

    import numpy as np

    out = dict(_drawn_inputs(seed))
    spreads = {'L0_tok_b': (0.0, 0.1),
     'L0_ffn_n1l_g': (1.0, 0.6),
     'L0_ffn_n1l_b': (0.0, 0.8),
     'L0_ffn_n1s_g': (1.0, 0.6),
     'L0_ffn_n1s_b': (0.0, 0.8),
     'L0_ffn_b_proj': (0.0, 0.1),
     'L0_ffn_n2l_g': (1.0, 0.6),
     'L0_ffn_n2l_b': (0.0, 2.0),
     'L0_ffn_n2s_g': (1.0, 0.6),
     'L0_ffn_n2s_b': (0.0, 2.0),
     'L0_ffn_b_fc1': (0.0, 0.736),
     'L0_ffn_b_fc2': (0.0, 0.1)}
    factors = {'L0_attn_b_proj': 2.973,
     'L0_ffn_gumbel_weights': 5.808,
     'L0_ffn_w_qkv': 3.054,
     'L0_ffn_w_proj': 2.929}
    for name, (base, spread) in spreads.items():
        noise = np.random.default_rng([zlib.crc32(name.encode()), seed]).standard_normal(out[name].shape)
        drawn = base * np.exp(spread * noise) if base else spread * noise
        out[name] = jnp.asarray(drawn.astype(out[name].dtype))
    for name, factor in factors.items():
        out[name] = (out[name] * factor).astype(out[name].dtype)
    return out
```

```python
import concourse.bass as bass
from concourse import mybir
from contextlib import ExitStack
import numpy as np

B, NTOK, D = 64, 197, 192
HEADS, HD = 12, 16
HID = 4 * D
NP, PS, CH, IMG = 14, 16, 3, 224
T = 99
TI = 2 * T
TP = 2 * TI
PAIRS = B // 2
LARGE = PAIRS // 2
HC = HID // 128
NPASS = 5
KEEP_CH = [D, D // 2, D // 3]
KEEP_HEADS = [HEADS, HEADS // 2, HEADS // 3]
IMW = 2 * PS + IMG * NP
EPS = 1e-5
HT_SLOTS = 9


def attention(x):
    steps = []
    for k in range(12):
        steps.append((x, "score", k))
        if k >= 2 and k % 2 == 0:
            steps.append((x, "pv", k // 2 - 1))
            if (k // 2 - 1) % 2 == 1:
                steps.append((x, "ot", (k // 2 - 1) // 2))
    return steps + [(x, "pv", 5), (x, "ot", 2)]


def split(x, n):
    return [(x, "split", n)] + [(x, "xT", 3 * n + c) for c in range(3)]


def project_in(x):
    return [(x, "qk", 0), (x, "qk", 1), (x, "qk", 2), (x, "stack", 0), (x, "v", 0), (x, "v", 1)]


def back(x):
    return [(x, "back", t) for t in range(4)]


def merge(a, b):
    out, j = [], 0
    for i, s in enumerate(a):
        out.append(s)
        while j < len(b) and (j + 1) * len(a) <= (i + 1) * len(b):
            out.append(b[j])
            j += 1
    return out + b[j:]


def mlp(branches):
    steps = []
    for n in range(branches):
        steps += [("b", "fc1", n * HC + m) for m in range(HC)]
        steps += [("b", "fc2", 2 * n), ("b", "fc2", 2 * n + 1)]
    return steps


A_HEAD = [("a", "img", 0), ("a", "tok", 0), ("a", "img", 1)]
A_IN = [("a", "tok", 1), ("a", "norm", 0)]
A_OUT = [("a", "proj", 0), ("a", "proj", 1)]
B_IN = [("b", "norm", 0)] + split("b", 0) + project_in("b")
B_MAX = [("b", "max", k) for k in range(12)] + [("b", "mrow", 0)]
B_OUT = [("b", "proj", 0), ("b", "proj", 1), ("b", "norm", 1)]


def order(kind, branches):
    att_a, att_b = attention("a"), attention("b")
    tail = split("b", 2) + mlp(branches) + [("b", "out", 0)]
    if kind == "a":
        return A_HEAD + A_IN + split("a", 0) + project_in("a") + att_a + back("a") + split("a", 1) + A_OUT
    if kind == "b":
        return B_IN + B_MAX + att_b + back("b") + split("b", 1) + B_OUT + tail
    cut = [att_b.index(("b", "ot", g)) + 1 for g in (0, 1)]
    return (A_HEAD + B_IN + A_IN + split("a", 0) + project_in("a") + B_MAX + att_a
            + att_b[:cut[0]] + back("a") + att_b[cut[0]:cut[1]] + split("a", 1) + att_b[cut[1]:]
            + back("b") + split("b", 1) + B_OUT + A_OUT + tail)


PHASES = [("a", 0, 1, -1), ("ab", 1, LARGE, 0), ("ab", 3, PAIRS - LARGE - 1, LARGE), ("b", 3, 1, PAIRS - 1)]
BANK_STEPS = ("tok", "xT", "qk", "v", "pv", "back", "proj", "mrow", "fc1", "fc2")
SCORE_STEPS = ("score", "max")


def signals(step, turn):
    x, what, n = step
    if what == "tok":
        return {"tok_made": 1, f"bank_read{turn}": 1}
    if what in ("xT", "v", "back", "proj", "mrow", "fc1", "fc2"):
        s = {f"bank_full{turn}": 1, f"bank_read{turn}": 1}
        if what == "back":
            s["rden_ready"] = 1
        if what == "mrow":
            s["mrow_in"] = 2 * 16
        return s
    if what == "qk":
        return {f"bank_full{turn}": 1, f"bank_read{turn}": 1, "qk_hi_ready": 1}
    if what == "pv":
        return {"pv_done": 1}
    if what == "ot":
        return {f"bank_read{turn}": 1}
    if what in SCORE_STEPS:
        return {f"score_full{turn}": 1, f"score_read{turn}": 1}
    if what == "img":
        return {"img_in": 6 * 16}
    if what == "norm":
        s = {"stats_ready": 2, "var_ready": 1, "rstd_ready": 1, "xn_ready": 1}
        if (x, n) == ("a", 0):
            s["hb_ready"] = 1
        if (x, n) == ("b", 0):
            s.update(y_ready=1, yb_ready=1)
        if (x, n) == ("b", 1):
            s.update(f_half=1, f_ready=1)
        return s
    if what == "split":
        return {"hi_ready": 1, "split_done": 3}
    if what == "stack":
        return {f"stack_in_{x}": 24 * 16}
    if what == "out":
        return {"out_done": 4 * 16}
    raise KeyError(what)


LEAD = {"out_done": 1, "f_ready": 1}


class Phase:

    def __init__(self, spec, start):
        self.kind, self.branches, self.count, self.first = spec
        self.steps = order(self.kind, self.branches)
        self.start = dict(start)
        self.turn, self.before, self.after = {}, {}, {}
        banks = scores = probs = 0
        so_far = {}
        for step in self.steps:
            x, what, n = step
            if what == "ot":
                self.turn[step] = self.turn[(x, "pv", 2 * n)]
            elif what == "pv" and n % 2 == 1:
                self.turn[step] = self.turn[(x, "pv", n - 1)]
            elif what in BANK_STEPS:
                self.turn[step] = banks % 4
                banks += 1
            elif what in SCORE_STEPS:
                self.turn[step] = scores % 2
                scores += 1
            self.before[step] = dict(so_far)
            for name, k in signals(step, self.turn.get(step)).items():
                so_far[name] = so_far.get(name, 0) + k
            self.after[step] = dict(so_far)
        self.per = so_far
        self.end = {k: self.start.get(k, 0) + self.count * so_far.get(k, 0) for k in {**start, **so_far}}

    def value(self, name, inside, it):
        base = self.start.get(name, 0) + inside
        per = self.per.get(name, 0)
        if self.count == 1 or per == 0:
            return base
        return (it - self.first) * per + base

    def upto(self, name, step, it, k=None):
        inside = self.after[step].get(name, 0) if k is None else self.before[step].get(name, 0) + k
        return self.value(name, inside, it)

    def ahead(self, name, step, it):
        v = self.value(name, self.before[step].get(name, 0), it)
        return None if isinstance(v, int) and v == 0 else v


def make_phases():
    phases, start = [], dict(LEAD)
    for spec in PHASES:
        phases.append(Phase(spec, start))
        start = phases[-1].end
    return phases


def passes(width):
    if width == D:
        return [(0, 0, 128, 0), (1, 0, 128, 1), (2, 0, 128, 2), (0, 0, 128, 3), (1, 64, 128, 4)]
    if width > 64:
        return [(0, 0, width, 0), (1, 0, 64, 1), (2, 0, width - 64, 2), (0, 0, width, 3)]
    return [(0, 0, width, 0), (1, 0, width, 1), (0, 0, width, 3)]


def build(nc, I, out):
    f32, f32r = mybir.dt.float32, mybir.dt.float32r
    ALU, ACT, AX = mybir.AluOpType, mybir.ActivationFunctionType, mybir.AxisListType
    phases = make_phases()
    with ExitStack() as ctx:
        def sb(name, shape, dt=f32):
            return ctx.enter_context(nc.sbuf_tensor(name, shape, dt))

        ident = sb("ident", [128, 128])
        ones = sb("ones", [1, 128])
        neg_half = sb("neg_half", [T, 8])
        pos = sb("pos", [T, 2, D])
        w_tok = sb("w_tok", [2 * CH * PS, PS // 2, D])
        w_in = {x: sb(f"w_in_{x}", [128, NPASS, 3 * D], f32r) for x in "ab"}
        w_out = {x: sb(f"w_out_{x}", [128, NPASS, D], f32r) for x in "ab"}
        w_fc1 = sb("w_fc1", [128, NPASS, HID], f32r)
        w_fc2 = sb("w_fc2", [128, HC, sum(KEEP_CH)])
        bias_qk = sb("bias_qk", [128, 3])
        bias_fc1 = sb("bias_fc1", [128, 3, HC])
        const_out = {x: sb(f"const_out_{x}", [T, D]) for x in "ab"}
        const_fc2 = sb("const_fc2", [T, D])
        gain = sb("gain", [128, 3])
        shift = sb("shift", [128, 3])
        v_bias = sb("v_bias", [128, 2])
        rows = sb("rows", [3, 2 * D])
        bout_row = sb("bout_row", [1, D])
        b2_row = sb("b2_row", [1, D])
        gum_row = sb("gum_row", [1, 3])
        gum_col = sb("gum_col", [3, 1])
        gum_all = sb("gum_all", [128, 3])
        fc1_raw = sb("fc1_raw", [128, HC])
        img = sb("img", [2 * CH * PS, IMW])
        xn = {x: sb(f"xn_{x}", [T, 4, D]) for x in "ab"}
        parts = {x: sb(f"parts_{x}", [128, 4 * 2 * D]) for x in "ab"}
        xT = {x: sb(f"xT_{x}", [128, 3, TP], f32r) for x in "ab"}
        qk_hi = {x: sb(f"qk_hi_{x}", [128, 3, TP]) for x in "ab"}
        q_st = {x: sb(f"q_st_{x}", [128, 6, TP], f32r) for x in "ab"}
        k_st = {x: sb(f"k_st_{x}", [128, 6, TP], f32r) for x in "ab"}
        vt = {x: sb(f"vt_{x}", [T, 4, HEADS, 32]) for x in "ab"}
        probs = sb("probs", [T, 4, 2, TP])
        h = sb("h", [T, 4, D])
        h2 = sb("h2", [T, 4, D])
        y = sb("y", [T, 4, D])
        x2 = sb("x2", [T, 4, D])
        hid = sb("hid", [128, HT_SLOTS, TP])
        stats = {x: sb(f"stats_{x}", [T, 4, 6]) for x in "ab"}
        mv = {x: sb(f"mv_{x}", [T, 4, 2]) for x in "ab"}
        ve = {x: sb(f"ve_{x}", [T, 2, 4]) for x in "ab"}
        rstd = {x: sb(f"rstd_{x}", [T, 2, 4]) for x in "ab"}
        rden = {x: sb(f"rden_{x}", [T, 4, HEADS]) for x in "ab"}
        carrier = sb("carrier", [1, 1 + len(LEAD)])
        neg_max = sb("neg_max", [T, 4, HEADS])
        max_rows = sb("max_rows", [HEADS, TP], f32r)
        xs = {x: parts[x][0:T, :].rearrange("p (t n) -> p t n", t=4) for x in "ab"}
        qk_lo = {x: parts[x][:, 0:3 * TP].rearrange("p (c n) -> p c n", c=3) for x in "ab"}
        oT = qk_hi
        stage = hid[:, :, :].rearrange("p s n -> p (s n)")

        one_row = hid[0:1, HT_SLOTS - 1, :]

        score_ps = ctx.enter_context(nc.psum_tensor("score_ps", [128, 4, 512], f32))
        bank = ctx.enter_context(nc.psum_tensor("bank", [128, 4, 512], f32))

        names = sorted({n for p in phases for n in p.end})
        sem = {n: ctx.enter_context(nc.semaphore(n)) for n in names}
        vec_chain = ctx.enter_context(nc.semaphore("vec_chain"))
        setup_in = ctx.enter_context(nc.semaphore("setup_in"))
        setup_sums = ctx.enter_context(nc.semaphore("setup_sums"))
        setup_done = ctx.enter_context(nc.semaphore("setup_done"))
        setup_link = ctx.enter_context(nc.semaphore("setup_link"))

        def slots(n):
            return stage[:, 0:3 * n].rearrange("p (s n) -> p s n", s=3)

        def raw(n, s):
            return stage[:, s * n:(s + 1) * n]

        def raw_hi(n):
            return stage[64:128, n:2 * n]

        TASKS = {0: ["tok", "in_a", "out_a", "const_a"], 1: ["in_b", "out_b", "const_b", "fc1", "fc2"],
                 2: ["in_b", "out_b", "const_b", "fc1", "fc2"], 3: []}

        def loads(k, task):
            set_ = "l" if k == 1 else "s"
            if task == "tok":
                return [(w_tok[:, :, :], I["w_tok"]), (pos[:, :, :], I["pos"]), (ident[:, :], I["ident"]),
                        (rows[0:2, 0:D], I["cls_b"]), (rows[0:2, D:D + D], I["tok_rows"][:, 0:D]),
                        (rden["a"][0:2, 0, 0:6], I["tok_rows"][:, D:TI])] + [
                            (k_st["b"][64 * e + 48:64 * e + 49, t, :].bitcast(f32), one_row) for e in range(2) for t in range(6)]
            if task == "in_a":
                return [(slots(3 * D), I["w_in_a"])]
            if task == "in_b":
                return [(slots(3 * D), I["w_in_b"]), (gain[:, :], I[f"n1{set_}_g"]), (shift[:, :], I[f"n1{set_}_b"])]
            if task == "out_a":
                return [(slots(D), I["w_out_a"]), (bout_row[:, :], I["b_out_a"])]
            if task == "out_b":
                more = [(rows[:, 0:D], I["keep_cols"]), (hid[0:3, 3, 0:3 * 128], I["keep_rows"]),
                        (gum_col[:, :], I["gum_col"])] if k == 2 else []
                return [(slots(D), I["w_out_b"]), (bout_row[:, :], I["b_out_b"]), (b2_row[:, :], I["b_fc2"])] + more
            if task == "fc1":
                return [(slots(HID), I["w_fc1"]), (gain[:, :], I[f"n2{set_}_g"]), (shift[:, :], I[f"n2{set_}_b"]),
                        (fc1_raw[:, :], I["b_fc1"])]
            if task == "fc2":
                return [(stage[:, 0:HC * D].rearrange("p (m n) -> p m n", m=HC), I["w_fc2"])] + (
                    [(gum_row[:, :], I["gum_row"])] if k == 2 else [])
            return []

        at_load, at_task, n_load, n_task = {}, {}, 0, 0
        for k in range(4):
            for task in TASKS[k]:
                n_load += 16 * len(loads(k, task))
                n_task += 1
                at_load[k, task], at_task[k, task] = n_load, n_task

        def setup_sync(sp, k):
            for task in TASKS[k]:
                if at_task[k, task] > 1:
                    sp.wait_ge(setup_done, at_task[k, task] - 1)
                for dst, src in loads(k, task):
                    sp.dma_start(dst, src).then_inc(setup_in, 16)

        def setup_tensor(pe, k):
            mm = nc.tensor.matmul
            for task in TASKS[k]:
                pe.wait_ge(setup_in, at_load[k, task])
                if at_task[k, task] > 1:
                    pe.wait_ge(setup_done, at_task[k, task] - 1)
                last = None
                if task == "tok":
                    pe.wait_ge(setup_link, 1)
                    mm(bank[0:T, 0, 0:D], rows[0:2, D:D + T], rows[0:2, 0:D], start=True, stop=True)
                    last = mm(bank[0:T, 0, D:2 * D], w_fc2[0:2, 0, 0:T], rows[0:2, 0:D], start=True, stop=True)
                if task == "in_b":
                    for c in range(3):
                        mm(bank[:, 1, c:c + 1], raw(576, 0)[:, c * 128:(c + 1) * 128], shift[:, 0:1], start=True, stop=False)
                        mm(bank[:, 1, c:c + 1], raw_hi(576)[:, c * 128:(c + 1) * 128], shift[64:128, 1:2], start=False, stop=True)
                    for c, n in ((0, 128), (1, 64)):
                        at = 2 * D + c * 128
                        mm(bank[128 - n:128, 2, c:c + 1], raw(576, 0)[:, at:at + n], shift[:, 0:1], start=True, stop=False)
                        last = mm(bank[128 - n:128, 2, c:c + 1], raw_hi(576)[:, at:at + n], shift[64:128, 1:2], start=False, stop=True)
                if task == "out_b" and k == 2:
                    pe.wait_ge(setup_link, link_at["cols"])
                    for s in range(3):
                        last = mm(bank[:, s, 0:D], hid[0:3, 3, s * 128:(s + 1) * 128], rows[0:3, 0:D], start=True, stop=True)
                if task in ("const_a", "const_b"):
                    last = mm(bank[0:T, 3, 0:D], ones[0:1, 0:T], bout_row[:, :], start=True, stop=task == "const_a")
                    if task == "const_b":
                        mm(bank[0:T, 3, 0:D], vbr(0), raw(D, 0), start=False, stop=False)
                        last = mm(bank[0:T, 3, 0:D], vbr(1), raw_hi(D), start=False, stop=True)
                if task == "fc1":
                    for n in range(phases[k].branches):
                        low = min(KEEP_CH[n], 128)
                        for m in range(HC):
                            at = bank[:, (0, 2, 3)[n], m:m + 1]
                            last = mm(at, stage[0:low, m * 128:(m + 1) * 128], shift[0:low, 0:1], start=True, stop=low < 128)
                            if low == 128:
                                last = mm(at, raw_hi(HID)[:, m * 128:(m + 1) * 128], shift[64:128, 1:2], start=False, stop=True)
                if task == "fc2":
                    last = mm(bank[0:T, 1, 0:D], ones[0:1, 0:T], b2_row[:, :], start=True, stop=True)
                    if k == 2:
                        last = mm(bank[:, 0, 0:3], ones[:, :], gum_row[:, :], start=True, stop=True)
                if last is not None:
                    last.then_inc(setup_sums, 1)

        def vbr(c):
            return stage[(0, 64)[c]:128, 3 * D + c * T:3 * D + (c + 1) * T]

        HAS_SUMS = {"tok", "in_b", "const_a", "const_b", "fc1", "fc2"}
        at_sums, n_sums = {}, 0
        for k in range(4):
            for task in TASKS[k]:
                n_sums += task in HAS_SUMS or (task == "out_b" and k == 2)
                at_sums[k, task] = n_sums
        link_at = {"cols": None}

        def setup_vector(v, k, links):
            def link(ins):
                links[0] += 1
                ins.then_inc(setup_link, 1)
                v.wait_ge(setup_link, links[0])

            def store(w, n):
                link(nc.vector.tensor_copy(w[:, 0:3, :], slots(n)))
                nc.vector.tensor_tensor(w[:, 3, :], raw(n, 0), w[:, 0, :].bitcast(f32), ALU.subtract)
                return nc.vector.tensor_tensor(w[64:128, 4, :], raw_hi(n), w[64:128, 1, :].bitcast(f32), ALU.subtract)

            for task in TASKS[k]:
                v.wait_ge(setup_in, at_load[k, task])
                if task == "tok":
                    link(tok_rows(v))
                if task == "out_b" and k == 2:
                    link(nc.vector.tensor_scalar(rows[:, 0:D], rows[:, 0:D], gum_col[:, 0:1], None, ALU.mult))
                if task in HAS_SUMS or (task == "out_b" and k == 2):
                    v.wait_ge(setup_sums, at_sums[k, task])
                if task == "tok":
                    last = nc.vector.tensor_tensor(pos[:, :, :], bank[0:T, 0, 0:2 * D].rearrange("p (u n) -> p u n", u=2),
                                                   pos[:, :, :], ALU.add)
                if task in ("in_a", "in_b"):
                    if task == "in_b":
                        nc.vector.tensor_scalar(bias_qk[0:64, :], bank[0:64, 1, 0:3], HD ** -0.5, None, ALU.mult)
                        nc.vector.tensor_copy(bias_qk[64:128, :], bank[64:128, 1, 0:3])
                        nc.vector.tensor_copy(v_bias[:, 0:1], bank[:, 2, 0:1])
                        nc.vector.tensor_copy(v_bias[64:128, 1:2], bank[64:128, 2, 1:2])
                        for s in range(3):
                            link(nc.vector.tensor_scalar(raw(576, s), raw(576, s), gain[:, s:s + 1], None, ALU.mult))
                    for s in range(3):
                        q = raw(576, s)[:, 0:2 * D].rearrange("p (c n) -> p c n", c=3)[:, :, 0:64]
                        link(nc.vector.tensor_scalar(q, q, HD ** -0.5, None, ALU.mult))
                    last = store(w_in[task[-1]], 3 * D)
                if task == "out_a":
                    last = store(w_out["a"], D)
                if task == "out_b":
                    if k == 2:
                        for s in range(3):
                            link(nc.vector.tensor_tensor(raw(D, s), bank[:, s, 0:D], raw(D, s), ALU.mult))
                        link(nc.vector.tensor_tensor(bout_row[:, :], bank[0:1, 0, 0:D], bout_row[:, :], ALU.mult))
                        link(nc.vector.tensor_tensor(b2_row[:, :], bank[0:1, 0, 0:D], b2_row[:, :], ALU.mult))
                    link(nc.vector.memset(stage[:, 3 * D:3 * D + 2 * T], 1.0))
                    for c in range(2):
                        link(nc.vector.tensor_scalar(vbr(c), vbr(c), v_bias[(0, 64)[c]:128, c:c + 1], None, ALU.mult))
                    last = store(w_out["b"], D)
                if task in ("const_a", "const_b"):
                    last = nc.vector.tensor_copy(const_out[task[-1]][:, :], bank[0:T, 3, 0:D])
                if task == "fc1":
                    for n in range(phases[k].branches):
                        nc.vector.tensor_tensor(bias_fc1[:, n, :], bank[:, (0, 2, 3)[n], 0:HC], fc1_raw[:, :], ALU.add)
                    for s in range(3):
                        link(nc.vector.tensor_scalar(raw(HID, s), raw(HID, s), gain[:, s:s + 1], None, ALU.mult))
                    last = store(w_fc1, HID)
                if task == "fc2":
                    src = stage[:, 0:HC * D].rearrange("p (m n) -> p m n", m=HC)
                    if k == 1:
                        nc.vector.tensor_copy(w_fc2[:, :, 0:D], src)
                    else:
                        link(nc.vector.tensor_copy(gum_all[:, :], bank[:, 0, 0:3]))
                        at = 0
                        for n in range(3):
                            nc.vector.tensor_scalar(w_fc2[:, :, at:at + KEEP_CH[n]], src[:, :, 0:KEEP_CH[n]],
                                                    gum_all[:, n:n + 1], None, ALU.mult)
                            at += KEEP_CH[n]
                    last = nc.vector.tensor_copy(const_fc2[:, :], bank[0:T, 1, 0:D])
                last.then_inc(setup_done, 1)

        def tok_rows(v):
            nc.vector.tensor_copy(w_fc2[0:2, 0, 0:D - T], rows[0:2, D + T:2 * D])
            return nc.vector.tensor_copy(w_fc2[0:2, 0, D - T:T], rden["a"][0:2, 0, 0:6])

        def count_links():
            n = 0
            for k in range(4):
                for task in TASKS[k]:
                    if task == "tok":
                        n += 1
                    if task == "out_b" and k == 2:
                        link_at["cols"] = n + 1
                        n += 1 + 5
                    if task == "in_a":
                        n += 3 + 1
                    if task == "in_b":
                        n += 3 + 3 + 1
                    if task == "out_a":
                        n += 1
                    if task == "out_b":
                        n += 1 + 2 + 1
                    if task == "fc1":
                        n += 3 + 1
                    if task == "fc2" and k == 2:
                        n += 1
        count_links()

        def tile_mm(dst, lhs, rhs, first, last):
            return nc.tensor.matmul(dst, lhs, rhs, start=first, stop=last)

        def by_feature(dst, x, w, col, width, n0=0, n=TP):
            ps = passes(width)
            for j, (c, r0, r1, s) in enumerate(ps):
                ins = tile_mm(dst, w[r0:r1, s, col:col + 128], xT[x][r0:r1, c, n0:n0 + n], j == 0, j == len(ps) - 1)
            return ins

        def by_token(dst, x, tt, w, col, n):
            ps = passes(D)
            for j, (c, r0, r1, s) in enumerate(ps):
                ins = tile_mm(dst, xT[x][r0:r1, c, tt * T:(tt + 1) * T], w[r0:r1, s, col:col + n], j == 0, j == len(ps) - 1)
            return ins

        def unit(n):
            g, i, hp = n // 4, (n // 2) % 2, n % 2
            return g, i, hp, 2 * g + hp

        def sync_step(sp, ph, step, it):
            x, what, n = step
            if what == "img":
                b = n if ph.kind == "a" else sp.snap(2 * (it + 1) + n)
                made = ph.ahead("tok_made", step, it)
                if made is not None:
                    sp.wait_ge(sem["tok_made"], made)
                for g in range(2):
                    for c in range(CH):
                        p = (g * CH + c) * PS
                        at = PS - g * (PS // 2)
                        sp.dma_start(img[p:p + PS, at:at + NP * IMG].rearrange("p (py w) -> p py w", w=IMG),
                                     I["x"][b, c].rearrange("(py ph) w -> ph py w", ph=PS)).then_inc(sem["img_in"], 16)
            if what == "stack":
                last = (x, "qk", 2)
                sp.wait_ge(sem[f"bank_read{ph.turn[last]}"], ph.upto(f"bank_read{ph.turn[last]}", last, it))
                v = ph.ahead("pv_done", step, it)
                if v is not None:
                    sp.wait_ge(sem["pv_done"], v)
                for side, dst, kinds in ((0, q_st, "hhl"), (1, k_st, "hlh")):
                    for b2 in range(2):
                        for e in range(2):
                            r = 16 * (side * 4 + b2 * 2 + e)
                            for g, kind in enumerate(kinds):
                                src = qk_hi[x] if kind == "h" else qk_lo[x]
                                to = 64 * e + 16 * g
                                sp.dma_start(dst[x][to:to + 16, 3 * b2:3 * b2 + 3, :].bitcast(f32), src[r:r + 16, :, :])\
                                    .then_inc(sem[f"stack_in_{x}"], 16)
            if what == "mrow":
                t = ph.turn[step]
                sp.wait_ge(sem[f"bank_read{t}"], ph.upto(f"bank_read{t}", step, it))
                for e in range(2):
                    sp.dma_start(q_st["b"][64 * e + 48:64 * e + 49, :, :].bitcast(f32),
                                 max_rows[6 * e:6 * e + 6, :].bitcast(f32)).then_inc(sem["mrow_in"], 16)

        def tensor_step(pe, ph, step, it):
            x, what, n = step
            t = ph.turn.get(step)

            def bank_free():
                v = ph.ahead(f"bank_read{t}", step, it)
                if v is not None:
                    pe.wait_ge(sem[f"bank_read{t}"], v)

            if what == "tok":
                bank_free()
                pe.wait_ge(sem["img_in"], ph.upto("img_in", ("a", "img", n), it))
                for u in range(2):
                    for j in range(PS // 2):
                        at = u * (T - 1) * PS + u * PS + j
                        ins = tile_mm(bank[0:T, t, u * D:(u + 1) * D], img[:, at:at + (T - 1) * PS + 1:PS],
                                      w_tok[:, j, :], j == 0, j == PS // 2 - 1)
                ins.then_inc(sem["tok_made"], 1)
            if what == "xT":
                bank_free()
                s = (x, "split", n // 3)
                pe.wait_ge(sem["split_done"], ph.upto("split_done", s, it))
                c = n % 3
                for tt in range(4):
                    ins = nc.tensor.transpose(bank[:, t, tt * T:(tt + 1) * T], xs[x][:, tt, c * 128:(c + 1) * 128], ident[0:T, 0:T])
                ins.then_inc(sem[f"bank_full{t}"], 1)
            if what in ("qk", "v", "proj", "fc1"):
                bank_free()
                which = {"qk": 0, "v": 0, "proj": 1, "fc1": 2}[what]
                for c in range(3):
                    st = (x, "xT", 3 * which + c)
                    pe.wait_ge(sem[f"bank_read{ph.turn[st]}"], ph.upto(f"bank_read{ph.turn[st]}", st, it))
                if what == "qk":
                    ins = by_feature(bank[:, t, 0:TP], x, w_in[x], n * 128, D)
                if what == "fc1":
                    ins = by_feature(bank[:, t, 0:TP], x, w_fc1, n % HC * 128, KEEP_CH[n // HC])
                if what in ("v", "proj"):
                    w, col = (w_in[x], 2 * D) if what == "v" else (w_out[x], 0)
                    for u in range(2):
                        ins = by_token(bank[0:T, t, u * D:(u + 1) * D], x, 2 * n + u, w, col, D)
                ins.then_inc(sem[f"bank_full{t}"], 1)
            if what in SCORE_STEPS:
                v = ph.ahead(f"score_read{t}", step, it)
                if v is not None:
                    pe.wait_ge(sem[f"score_read{t}"], v)
                pe.wait_ge(sem[f"stack_in_{x}"], ph.upto(f"stack_in_{x}", (x, "stack", 0), it))
                if what == "score" and x == "b":
                    pe.wait_ge(sem["mrow_in"], ph.upto("mrow_in", ("b", "mrow", 0), it))
                g, i, hp, tile = unit(n)
                rows_ = 49 if (what, x) == ("score", "b") else 48
                left, right = (k_st, q_st) if what == "score" else (q_st, k_st)
                for u in range(2):
                    for e in range(2):
                        r = slice(64 * e, 64 * e + rows_)
                        ins = tile_mm(score_ps[0:T, 2 * t + e, u * TI:(u + 1) * TI],
                                      left[x][r, tile, i * TI + u * T:i * TI + (u + 1) * T],
                                      right[x][r, tile, i * TI:(i + 1) * TI], True, True)
                ins.then_inc(sem[f"score_full{t}"], 1)
            if what == "pv":
                g, i = n // 2, n % 2
                if i == 0:
                    bank_free()
                for hp in range(2):
                    st = (x, "score", 2 * n + hp)
                    pe.wait_ge(sem[f"score_read{ph.turn[st]}"], ph.upto(f"score_read{ph.turn[st]}", st, it))
                st = (x, "v", i)
                pe.wait_ge(sem[f"bank_read{ph.turn[st]}"], ph.upto(f"bank_read{ph.turn[st]}", st, it))
                for u in range(2):
                    keys = T - u
                    for hp in range(2):
                        for e in range(2):
                            qd = 2 * hp + e
                            ins = tile_mm(bank[32 * qd:32 * qd + 32, t, i * TI:(i + 1) * TI],
                                          vt[x][0:keys, 2 * i + u, 4 * g + qd, :],
                                          probs[0:keys, (2 * n + hp) % 4, e, u * TI:(u + 1) * TI], u == 0, u == 1)
                ins.then_inc(sem["pv_done"], 1)
            if what == "back":
                bank_free()
                st = (x, "ot", 2)
                pe.wait_ge(sem[f"bank_read{ph.turn[st]}"], ph.upto(f"bank_read{ph.turn[st]}", st, it))
                for g in range(3):
                    ins = nc.tensor.transpose(bank[0:T, t, g * 128:(g + 1) * 128], oT[x][:, g, n * T:(n + 1) * T], ident[:, :])
                ins.then_inc(sem[f"bank_full{t}"], 1)
            if what == "mrow":
                bank_free()
                for k in (10, 11):
                    st = ("b", "max", k)
                    pe.wait_ge(sem[f"score_read{ph.turn[st]}"], ph.upto(f"score_read{ph.turn[st]}", st, it))
                for tt in range(4):
                    ins = nc.tensor.transpose(bank[0:HEADS, t, tt * T:(tt + 1) * T], neg_max[:, tt, :], ident[0:T, 0:T])
                ins.then_inc(sem[f"bank_full{t}"], 1)
            if what == "fc2":
                bank_free()
                br, i = n // 2, n % 2
                st = ("b", "fc1", br * HC + HC - 1)
                for m in range(HC):
                    st = ("b", "fc1", br * HC + m)
                    pe.wait_ge(sem[f"bank_read{ph.turn[st]}"], ph.upto(f"bank_read{ph.turn[st]}", st, it))
                width, at = KEEP_CH[br], sum(KEEP_CH[:br])
                for u in range(2):
                    tt = 2 * i + u
                    for m in range(HC):
                        ins = tile_mm(bank[0:T, t, u * D:u * D + width], hid[:, (br * HC + m) % HT_SLOTS, tt * T:(tt + 1) * T],
                                      w_fc2[:, m, at:at + width], m == 0, m == HC - 1)
                ins.then_inc(sem[f"bank_full{t}"], 1)

        def full(eng, ph, step, it):
            t = ph.turn[step]
            eng.wait_ge(sem[f"bank_full{t}"], ph.upto(f"bank_full{t}", step, it))
            return t

        def scalar_step(act, ph, step, it):
            x, what, n = step
            if what == "split":
                wait_xn(act, ph, step, it)
                nc.scalar.activation(xs[x][:, :, 0:128].bitcast(f32r), xn[x][:, :, 0:128], ACT.Identity)
                nc.scalar.activation(xs[x][:, :, 192:256].bitcast(f32r), xn[x][:, :, 128:D], ACT.Identity)\
                    .then_inc(sem["hi_ready"], 1)
            if what == "xT" and n % 3 != 1:
                t = full(act, ph, step, it)
                nc.scalar.activation(xT[x][:, n % 3, :], bank[:, t, 0:TP], ACT.Identity).then_inc(sem[f"bank_read{t}"], 1)
            if what == "qk":
                t = full(act, ph, step, it)
                bias = bias_qk[:, n:n + 1] if x == "b" else 0.0
                nc.scalar.activation(qk_hi[x][:, n, :].bitcast(f32r), bank[:, t, 0:TP], ACT.Identity, bias=bias)\
                    .then_inc(sem["qk_hi_ready"], 1)
            if what == "v":
                t = full(act, ph, step, it)
                nc.scalar.activation(vt[x][:, 2 * n:2 * n + 2, :, 0:HD],
                                     bank[0:T, t, 0:2 * D].rearrange("p (u h d) -> p u h d", u=2, h=HEADS),
                                     ACT.Identity).then_inc(sem[f"bank_read{t}"], 1)
            if what == "score":
                t = ph.turn[step]
                act.wait_ge(sem[f"score_full{t}"], ph.upto(f"score_full{t}", step, it))
                v = ph.upto("pv_done", (x, "pv", (n - 4) // 2), it) if n >= 4 else ph.ahead("pv_done", step, it)
                if v is not None:
                    act.wait_ge(sem["pv_done"], v)
                func, bias = (ACT.Square, 1.0) if x == "a" else (ACT.Exp, 0.0)
                nc.scalar.activation(probs[:, n % 4, :, :], score_ps[0:T, 2 * t:2 * t + 2, 0:TP], func, bias=bias)\
                    .then_inc(sem[f"score_read{t}"], 1)
            if what == "mrow":
                t = full(act, ph, step, it)
                nc.scalar.activation(max_rows[:, :], bank[0:HEADS, t, 0:TP], ACT.Identity).then_inc(sem[f"bank_read{t}"], 1)
            if what == "fc1":
                t = full(act, ph, step, it)
                if n >= HT_SLOTS:
                    for i in range(2):
                        st = ("b", "fc2", 2 * ((n - HT_SLOTS) // HC) + i)
                        act.wait_ge(sem[f"bank_full{ph.turn[st]}"], ph.upto(f"bank_full{ph.turn[st]}", st, it))
                nc.scalar.activation(hid[:, n % HT_SLOTS, :], bank[:, t, 0:TP], ACT.Gelu,
                                     bias=bias_fc1[:, n // HC, n % HC:n % HC + 1]).then_inc(sem[f"bank_read{t}"], 1)
            if what == "out":
                for i in range(2):
                    st = ("b", "fc2", 2 * ph.branches - 2 + i)
                    act.wait_ge(sem[f"bank_read{ph.turn[st]}"], ph.upto(f"bank_read{ph.turn[st]}", st, it))
                for i in range(2):
                    for u in range(2):
                        act.dma_start(out[2 * it + i, u * T:u * T + T - u, :], x2[0:T - u, 2 * i + u, :])\
                            .then_inc(sem["out_done"], 16)

        def wait_xn(eng, ph, step, it):
            x, _, n = step
            if n == 1:
                st = (x, "back", 3)
                t = ph.turn[st]
                eng.wait_ge(sem[f"bank_read{t}"], ph.upto(f"bank_read{t}", st, it))
            else:
                eng.wait_ge(sem["xn_ready"], ph.upto("xn_ready", (x, "norm", n // 2), it))

        def pool_step(pool, ph, step, it):
            x, what, n = step
            if what == "norm":
                pool.wait_ge(sem["var_ready"], ph.upto("var_ready", step, it))
                nc.gpsimd.tensor_tensor(rstd[x][:, :, :], ve[x][:, :, :], neg_half[:, :].rearrange("p (a b) -> p a b", a=2),
                                        ALU.pow).then_inc(sem["rstd_ready"], 1)
                if (x, n) == ("a", 0):
                    pool.wait_ge(sem["xn_ready"], ph.upto("xn_ready", step, it))
                    nc.gpsimd.tensor_tensor(h[:, :, :], h[:, :, :], const_out["a"][:, :].unsqueeze(1).to_broadcast([T, 4, D]),
                                            ALU.add).then_inc(sem["hb_ready"], 1)
                if (x, n) == ("b", 0):
                    pool.wait_ge(sem["y_ready"], ph.upto("y_ready", step, it))
                    nc.gpsimd.tensor_tensor(y[:, :, :], y[:, :, :], const_out["b"][:, :].unsqueeze(1).to_broadcast([T, 4, D]),
                                            ALU.add).then_inc(sem["yb_ready"], 1)
                if (x, n) == ("b", 1):
                    pool.wait_ge(sem["xn_ready"], ph.upto("xn_ready", step, it))
                    nc.gpsimd.tensor_tensor(x2[:, :, :], x2[:, :, :], h2[:, :, :], ALU.add).then_inc(sem["f_half"], 1)
                    pool.wait_ge(sem["f_half"], ph.upto("f_half", step, it))
                    nc.gpsimd.tensor_tensor(x2[:, :, :], x2[:, :, :], const_fc2[:, :].unsqueeze(1).to_broadcast([T, 4, D]),
                                            ALU.add).then_inc(sem["f_ready"], 1)
            if what == "split":
                pool.wait_ge(sem["hi_ready"], ph.upto("hi_ready", step, it))
                nc.gpsimd.tensor_tensor(xs[x][:, :, 128:192].bitcast(f32r), xn[x][:, :, 0:64], xs[x][:, :, 0:64], ALU.subtract)\
                    .then_inc(sem["split_done"], 1)
                nc.gpsimd.tensor_tensor(xs[x][:, :, 256:320].bitcast(f32r), xn[x][:, :, 64:128], xs[x][:, :, 64:128], ALU.subtract)\
                    .then_inc(sem["split_done"], 1)
                nc.gpsimd.tensor_tensor(xs[x][:, :, 320:384].bitcast(f32r), xn[x][:, :, 128:D], xs[x][:, :, 192:256], ALU.subtract)\
                    .then_inc(sem["split_done"], 1)

        def vector_step(v, ph, step, it):
            x, what, n = step
            if what == "tok":
                t = ph.turn[step]
                v.wait_ge(sem["tok_made"], ph.upto("tok_made", step, it))
                nc.vector.tensor_tensor(h[:, 2 * n:2 * n + 2, :], bank[0:T, t, 0:2 * D].rearrange("p (u n) -> p u n", u=2),
                                        pos[:, :, :], ALU.add).then_inc(sem[f"bank_read{t}"], 1)
            if what == "norm":
                src = {("a", 0): h, ("b", 0): h2, ("b", 1): x2}[x, n]
                if (x, n) == ("a", 0):
                    wait_own(v, ph, [("a", "tok", i) for i in range(2)], it)
                if (x, n) == ("b", 0):
                    for s in range(4):
                        val = ph.ahead(f"bank_read{s}", ph.steps[0], it)
                        if val is not None:
                            v.wait_ge(sem[f"bank_read{s}"], val)
                if (x, n) == ("b", 1):
                    wait_own(v, ph, [("b", "proj", i) for i in range(2)], it)
                for tt in range(4):
                    ins = nc.vector.bn_stats(stats[x][:, tt, :], src[:, tt, :])
                ins.then_inc(sem["stats_ready"], 1)
                v.wait_ge(sem["stats_ready"], ph.upto("stats_ready", step, it, 1))
                nc.vector.memset(carrier[:, 0:1], 0.0)
                for tt in range(4):
                    ins = nc.vector.bn_aggr(mv[x][:, tt, :], stats[x][:, tt, :])
                ins.then_inc(sem["stats_ready"], 1)
                v.wait_ge(sem["stats_ready"], ph.upto("stats_ready", step, it, 2))
                var = mv[x][:, :, 1]
                nc.vector.tensor_scalar(ve[x][:, 0, :], var, EPS, None, ALU.add)
                two = (1.0 + EPS, EPS * EPS) if (x, n) == ("b", 0) else (1.0, EPS)
                nc.vector.tensor_scalar(ve[x][:, 1, :], var, two[0], two[1], ALU.mult, ALU.add).then_inc(sem["var_ready"], 1)
                v.wait_ge(sem["rstd_ready"], ph.upto("rstd_ready", step, it))
                if (x, n) == ("b", 0):
                    for tt in range(4):
                        ins = nc.vector.tensor_scalar(y[:, tt, :], src[:, tt, :], mv[x][:, tt, 0:1], rstd[x][:, 0, tt:tt + 1],
                                                      ALU.subtract, ALU.mult)
                    ins.then_inc(sem["y_ready"], 1)
                for tt in range(4):
                    ins = nc.vector.tensor_scalar(xn[x][:, tt, :], src[:, tt, :], mv[x][:, tt, 0:1], rstd[x][:, 1, tt:tt + 1],
                                                  ALU.subtract, ALU.mult)
                ins.then_inc(sem["xn_ready"], 1)
            if what == "xT" and n % 3 == 1:
                t = full(v, ph, step, it)
                nc.vector.tensor_copy(xT[x][:, 1, :], bank[:, t, 0:TP]).then_inc(sem[f"bank_read{t}"], 1)
            if what == "qk":
                t = ph.turn[step]
                v.wait_ge(sem["qk_hi_ready"], ph.upto("qk_hi_ready", step, it))
                bias = bias_qk[:, n:n + 1] if x == "b" else 0.0
                nc.vector.scalar_tensor_tensor(qk_lo[x][:, n, :].bitcast(f32r), bank[:, t, 0:TP], bias, qk_hi[x][:, n, :],
                                               ALU.add, ALU.subtract).then_inc(sem[f"bank_read{t}"], 1)
            if what == "max":
                t = ph.turn[step]
                g, i, hp, tile = unit(n)
                v.wait_ge(sem[f"score_full{t}"], ph.upto(f"score_full{t}", step, it))
                dst = neg_max[:, 2 * i:2 * i + 2, :].rearrange("p u (e t) -> p e u t", e=2)[:, :, :, tile]
                src = score_ps[0:T, 2 * t:2 * t + 2, 0:TP].rearrange("p e (u k) -> p e u k", u=2)[:, :, :, 0:NTOK]
                nc.vector.tensor_reduce(dst, src, AX.X, ALU.max, negate=True).then_inc(sem[f"score_read{t}"], 1)
            if what == "ot":
                t = ph.turn[step]
                v.wait_ge(sem["pv_done"], ph.upto("pv_done", (x, "pv", 2 * n + 1), it))
                if x == "a":
                    for i in range(2):
                        ins = nc.vector.tensor_scalar(oT[x][:, n, i * TI:(i + 1) * TI], bank[:, t, i * TI:(i + 1) * TI],
                                                      bank[:, t, (i + 1) * TI - 1:(i + 1) * TI], None, ALU.add)
                else:
                    ins = nc.vector.tensor_copy(oT[x][:, n, :], bank[:, t, 0:TP])
                ins.then_inc(sem[f"bank_read{t}"], 1)
            if what == "back":
                t = full(v, ph, step, it)
                o = bank[0:T, t, 0:3 * 128].rearrange("p (h d) -> p h d", h=HEADS)
                nc.vector.reciprocal(rden[x][:, n, :], o[:, :, HD]).then_inc(sem["rden_ready"], 1)
                v.wait_ge(sem["rden_ready"], ph.upto("rden_ready", step, it))
                nc.vector.tensor_tensor(xn[x][:, n, :].rearrange("p (h d) -> p h d", h=HEADS), o[:, :, 0:HD],
                                        rden[x][:, n, :].unsqueeze(2).to_broadcast([T, HEADS, HD]), ALU.mult)\
                    .then_inc(sem[f"bank_read{t}"], 1)
            if what == "proj":
                t = full(v, ph, step, it)
                if x == "a":
                    v.wait_ge(sem["hb_ready"], ph.upto("hb_ready", ("a", "norm", 0), it))
                    val = ph.ahead("f_ready", step, it)
                    if val is not None:
                        v.wait_ge(sem["f_ready"], val)
                    dst, src = h2, h
                else:
                    v.wait_ge(sem["yb_ready"], ph.upto("yb_ready", ("b", "norm", 0), it))
                    val = ph.ahead("out_done", step, it)
                    if val is not None:
                        v.wait_ge(sem["out_done"], val)
                    dst, src = x2, y
                nc.vector.tensor_tensor(dst[:, 2 * n:2 * n + 2, :], bank[0:T, t, 0:2 * D].rearrange("p (u n) -> p u n", u=2),
                                        src[:, 2 * n:2 * n + 2, :], ALU.add).then_inc(sem[f"bank_read{t}"], 1)
            if what == "fc2":
                t = full(v, ph, step, it)
                br, i = n // 2, n % 2
                v.wait_ge(sem["f_ready"], ph.upto("f_ready", ("b", "norm", 1), it))
                if br:
                    wait_own(v, ph, [("b", "fc2", n - 2)], it)
                w = KEEP_CH[br]
                acc = x2[:, 2 * i:2 * i + 2, 0:w]
                nc.vector.tensor_tensor(acc, bank[0:T, t, 0:2 * D].rearrange("p (u n) -> p u n", u=2)[:, :, 0:w],
                                        acc, ALU.add).then_inc(sem[f"bank_read{t}"], 1)

        def wait_own(eng, ph, steps, it):
            for st in steps:
                t = ph.turn[st]
                eng.wait_ge(sem[f"bank_read{t}"], ph.upto(f"bank_read{t}", st, it))

        def run(eng, ph, do):
            if ph.count > 1:
                with eng.Fori(ph.first, ph.first + ph.count) as it:
                    for step in ph.steps:
                        do(eng, ph, step, it)
            else:
                for step in ph.steps:
                    do(eng, ph, step, ph.first)

        links = [0]
        init = ctx.enter_context(nc.semaphore("init"))
        for k, ph in enumerate(phases):
            with nc.Block() as block:
                @block.sync
                def _(sp):
                    if k == 0:
                        sp.wait_ge(init, 6)
                    setup_sync(sp, k)
                    run(sp, ph, sync_step)

                @block.gpsimd
                def _(pool):
                    if k == 0:
                        nc.gpsimd.memset(neg_half[:, :], -0.5).then_inc(init, 1)
                        nc.gpsimd.memset(vt["a"][:, :, :, :], 1.0).then_inc(init, 1)
                        nc.gpsimd.memset(vt["b"][:, :, :, :], 1.0).then_inc(init, 1)
                        nc.gpsimd.memset(img[:, :], 0.0).then_inc(init, 1)
                        nc.gpsimd.memset(one_row, 1.0).then_inc(init, 1)
                        pool.wait_ge(init, 6)
                    run(pool, ph, pool_step)

                @block.vector
                def _(v):
                    if k == 0:
                        nc.vector.memset(ones[:, :], 1.0).then_inc(init, 1)
                        for at, (name, lead) in enumerate(LEAD.items()):
                            nc.vector.memset(carrier[:, 1 + at:2 + at], 0.0).then_inc(sem[name], lead)
                    setup_vector(v, k, links)
                    run(v, ph, vector_step)

                @block.scalar
                def _(act):
                    if k == 0:
                        act.wait_ge(init, 6)
                    if TASKS[k]:
                        act.wait_ge(setup_done, at_task[k, TASKS[k][-1]])
                    run(act, ph, scalar_step)
                    if k == len(phases) - 1:
                        act.wait_ge(sem["out_done"], ph.end["out_done"])

                @block.tensor
                def _(pe):
                    if k == 0:
                        pe.wait_ge(init, 6)
                    setup_tensor(pe, k)
                    if TASKS[k]:
                        pe.wait_ge(setup_done, at_task[k, TASKS[k][-1]])
                    run(pe, ph, tensor_step)


def kernel(**inputs):
    import concourse.bacc as bacc
    from concourse.bass_utils import run_bass_kernel_spmd

    def get(name):
        return np.asarray(inputs[name])

    def stack(w):
        w = w.reshape(D, -1)
        return np.ascontiguousarray(np.stack([w[0:128], np.concatenate([w[0:64], w[128:192]]), w[64:192]], 1))

    cols = [side * D + (2 * (b2 * 3 + c) + e) * HD + d
            for c in range(3) for side in range(2) for b2 in range(2) for e in range(2) for d in range(HD)]
    cols += list(range(2 * D, 3 * D))
    f = np.float32
    pos = np.zeros((TI, D), f)
    pos[:NTOK] = get("L0_tok_pos_embed")
    tok_rows = np.zeros((2, TI), f)
    tok_rows[0, 0] = 1.0
    tok_rows[1, 1:NTOK] = 1.0
    w_tok = get("L0_tok_W").reshape(D, CH, PS, 2, PS // 2).transpose(3, 1, 2, 4, 0).reshape(2 * CH * PS, PS // 2, D)
    keep_rows = np.zeros((3, 3, 128), f)
    row_of = stack(np.arange(D))[:, :, 0].T
    for n in range(3):
        keep_rows[n] = row_of < KEEP_HEADS[n] * HD
    keep_cols = np.array([[c < KEEP_CH[n] for c in range(D)] for n in range(3)], f)
    gum = get("L0_ffn_gumbel_weights")
    arrays = {
        "x": get("x"), "w_tok": w_tok, "pos": pos.reshape(2, T, D).transpose(1, 0, 2), "ident": np.eye(128, dtype=f),
        "cls_b": np.stack([get("L0_tok_class_token")[0], get("L0_tok_b")]), "tok_rows": tok_rows,
        "w_in_a": stack(get("L0_attn_w_qkv")[:, cols]), "w_out_a": stack(get("L0_attn_w_proj")),
        "b_out_a": get("L0_attn_b_proj")[None],
        "w_in_b": stack(get("L0_ffn_w_qkv")[:, cols]), "w_out_b": stack(get("L0_ffn_w_proj")),
        "b_out_b": get("L0_ffn_b_proj")[None],
        "w_fc1": stack(get("L0_ffn_w_fc1")), "b_fc1": get("L0_ffn_b_fc1").reshape(HC, 128).T,
        "w_fc2": get("L0_ffn_w_fc2").reshape(HC, 128, D).transpose(1, 0, 2), "b_fc2": get("L0_ffn_b_fc2")[None],
        "keep_rows": keep_rows.reshape(3, 3 * 128), "keep_cols": keep_cols,
        "gum_col": gum[:, None], "gum_row": gum[None],
    }
    for name in ("n1l", "n1s", "n2l", "n2s"):
        for part in "gb":
            arrays[f"{name}_{part}"] = stack(get(f"L0_ffn_{name}_{part}"))[:, :, 0]
    arrays = {k: np.ascontiguousarray(v) for k, v in arrays.items()}
    nc = bacc.Bacc("TRN2", target_bir_lowering=False, num_devices=1)
    given = {k: nc.dram_tensor(f"in_{k}", v.shape, mybir.dt.from_np(v.dtype), kind="ExternalInput").ap()
             for k, v in arrays.items()}
    out = nc.dram_tensor("out", (B, NTOK, D), mybir.dt.float32, kind="ExternalOutput").ap()
    build(nc, given, out)
    r = run_bass_kernel_spmd(nc, [{f"in_{k}": v for k, v in arrays.items()}], core_ids=[0])
    return r.results[0]["out"]
```

```python
import concourse.bass as bass
from concourse import mybir
from contextlib import ExitStack
import numpy as np

B, NTOK, D = 64, 197, 192
HEADS, HD = 12, 16
HID = 4 * D
NP, PS, CH, IMG = 14, 16, 3, 224
T = 99
TI = 2 * T
TP = 2 * TI
PAIRS = B // 2
LARGE = PAIRS // 2
HC = HID // 128
NPASS = 5
KEEP_CH = [D, D // 2, D // 3]
KEEP_HEADS = [HEADS, HEADS // 2, HEADS // 3]
IMW = 2 * PS + IMG * NP
EPS = 1e-5
HT_SLOTS = 9


def attention(x):
    steps = []
    for k in range(12):
        steps.append((x, "score", k))
        if k >= 2 and k % 2 == 0:
            steps.append((x, "pv", k // 2 - 1))
            if (k // 2 - 1) % 2 == 1:
                steps.append((x, "ot", (k // 2 - 1) // 2))
    return steps + [(x, "pv", 5), (x, "ot", 2)]


def transposes(x, n):
    return [(x, "xT", 3 * n + c) for c in range(3)]


def project_in(x):
    return transposes(x, 0) + [(x, "qk", c) for c in range(3)] + [(x, "stack", 0), (x, "v", 0), (x, "v", 1)]


def back(x):
    return [(x, "back", t) for t in range(4)]


def merge(a, b):
    out, j = [], 0
    for i, s in enumerate(a):
        out.append(s)
        while j < len(b) and (j + 1) * len(a) <= (i + 1) * len(b):
            out.append(b[j])
            j += 1
    return out + b[j:]


def mlp(branches):
    steps = []
    for n in range(branches):
        steps += [("b", "fc1", n * HC + m) for m in range(HC)]
        steps += [("b", "fc2", 2 * n), ("b", "fc2", 2 * n + 1)]
    return steps


def body(branches):
    att_a, att_b, maxes, fc = attention("a"), attention("b"), [("b", "max", k) for k in range(12)], mlp(branches)

    def at(att, kind, k):
        return [s[1:] for s in att].index((kind, k)) + 1

    a8, b3, b7 = at(att_a, "score", 7), at(att_b, "score", 2), at(att_b, "score", 6)
    return ([("a", "img", 0), ("b", "const", 0)] + project_in("b") + project_in("a") + [("a", "tok", 0), ("a", "img", 1)]
            + maxes[:4] + merge(maxes[4:], att_a[:a8]) + [("b", "mrow", 0)] + att_a[a8:]
            + back("a") + att_b[:b3] + [("a", "split", 1)] + att_b[b3:]
            + back("b") + [("b", "split", 1)] + transposes("a", 1) + [("a", "proj", 0), ("a", "proj", 1)]
            + transposes("b", 1) + [("b", "proj", 0), ("b", "proj", 1), ("a", "tok", 1), ("b", "norm", 1)]
            + [("b", "split", 2), ("b", "sum", 0)] + transposes("b", 2) + fc[:2]
            + [("b", "norm", 0)] + fc[2:4] + [("b", "split", 0)] + fc[4:6]
            + [("a", "norm", 0), ("a", "split", 0)] + fc[6:] + [("b", "out", 0)])


A_HEAD = [("a", "img", 0), ("a", "tok", 0), ("a", "img", 1), ("a", "tok", 1), ("a", "norm", 0), ("a", "split", 0)]
B_NEXT = [("b", "norm", 0), ("b", "split", 0)]


def order(kind, branches):
    if kind == "first":
        return A_HEAD
    steps = body(branches)
    if kind == "a":
        return [s for s in steps if s[0] == "a" or s in B_NEXT]
    if kind == "b":
        return [s for s in steps if s[0] == "b" and s not in B_NEXT]
    if kind == "last":
        return [s for s in steps if s not in A_HEAD]
    return steps


PHASES = [("first", 0, 1, -2), ("a", 0, 1, -1), ("ab", 1, LARGE, 0), ("ab", 3, PAIRS - LARGE - 2, LARGE),
          ("last", 3, 1, PAIRS - 2), ("b", 3, 1, PAIRS - 1)]
LARGE_PHASE, SMALL = 2, 3
BANK_STEPS = ("tok", "xT", "qk", "v", "pv", "back", "proj", "mrow", "fc1", "fc2")
SCORE_STEPS = ("score", "max")


def signals(step, turn):
    x, what, n = step
    if what == "tok":
        return {"tok_made": 1, f"bank_read{turn}": 1}
    if what in ("xT", "v", "back", "proj", "mrow", "fc1", "fc2"):
        s = {f"bank_full{turn}": 1, f"bank_read{turn}": 1}
        if what == "back":
            s["rden_ready"] = 1
        if what == "mrow":
            s["mrow_in"] = 2 * 16
        return s
    if what == "qk":
        return {f"bank_full{turn}": 1, f"bank_read{turn}": 1, "qk_hi_ready": 1}
    if what == "pv":
        return {"pv_done": 1}
    if what == "ot":
        return {f"bank_read{turn}": 1}
    if what in SCORE_STEPS:
        return {f"score_full{turn}": 1, f"score_read{turn}": 1}
    if what == "img":
        return {"img_in": 6 * 16}
    if what == "norm":
        s = {"stats_ready": 2, "var_ready": 1, "rstd_ready": 1, "xn_ready": 1}
        if (x, n) == ("a", 0):
            s["hb_ready"] = 1
        if (x, n) == ("b", 0):
            s.update(y_ready=1, hc_ready=1)
        return s
    if what == "split":
        return {"hi_ready": 1, f"split_done_{x}": 3}
    if what == "sum":
        return {"f_half": 1, "f_ready": 1}
    if what == "const":
        return {"yb_ready": 1}
    if what == "stack":
        return {f"stack_in_{x}": 12 * 16}
    if what == "out":
        return {"out_done": 4 * 16}
    raise KeyError(what)


LEAD = {"out_done": 1}


class Phase:

    def __init__(self, spec, start):
        self.kind, self.branches, self.count, self.first = spec
        self.steps = order(self.kind, self.branches)
        self.start = dict(start)
        self.turn, self.before, self.after = {}, {}, {}
        self.pos = {step: i for i, step in enumerate(self.steps)}
        self.weights = [step for step in self.steps if step[1] == "score"]
        banks = scores = 0
        so_far = {}
        for step in self.steps:
            x, what, n = step
            if what == "ot":
                self.turn[step] = self.turn[(x, "pv", 2 * n)]
            elif what == "pv" and n % 2 == 1:
                self.turn[step] = self.turn[(x, "pv", n - 1)]
            elif what in BANK_STEPS:
                self.turn[step] = banks % 4
                banks += 1
            elif what in SCORE_STEPS:
                self.turn[step] = scores % 2
                scores += 1
            self.before[step] = dict(so_far)
            for name, k in signals(step, self.turn.get(step)).items():
                so_far[name] = so_far.get(name, 0) + k
            self.after[step] = dict(so_far)
        self.per = so_far
        self.end = {k: self.start.get(k, 0) + self.count * so_far.get(k, 0) for k in {**start, **so_far}}

    def value(self, name, inside, it):
        base = self.start.get(name, 0) + inside
        per = self.per.get(name, 0)
        if self.count == 1 or per == 0:
            return base
        return (it - self.first) * per + base

    def upto(self, name, step, it, k=None):
        inside = self.after[step].get(name, 0) if k is None else self.before[step].get(name, 0) + k
        return self.value(name, inside, it)

    def seen(self, name, by, step, it, k=None):
        if by in self.pos and self.pos[by] < self.pos[step]:
            return self.upto(name, by, it, k)
        if self.count == 1:
            return self.start.get(name) or None
        inside = self.after[by].get(name, 0) if k is None else self.before[by].get(name, 0) + k
        assert self.start[name] + inside > self.per[name]
        return self.value(name, inside - self.per[name], it)

    def ahead(self, name, step, it):
        v = self.value(name, self.before[step].get(name, 0), it)
        return None if isinstance(v, int) and v == 0 else v


def make_phases():
    phases, start = [], dict(LEAD)
    for spec in PHASES:
        phases.append(Phase(spec, start))
        start = phases[-1].end
    return phases


def passes(width):
    if width == D:
        return [(0, 0, 128, 0), (1, 0, 128, 1), (2, 0, 128, 2), (0, 0, 128, 3), (1, 64, 128, 4)]
    if width > 64:
        return [(0, 0, width, 0), (1, 0, 64, 1), (2, 0, width - 64, 2), (0, 0, width, 3)]
    return [(0, 0, width, 0), (1, 0, width, 1), (0, 0, width, 3)]


def build(nc, I, out):
    f32, f32r = mybir.dt.float32, mybir.dt.float32r
    ALU, ACT, AX = mybir.AluOpType, mybir.ActivationFunctionType, mybir.AxisListType
    phases = make_phases()
    with ExitStack() as ctx:
        def sb(name, shape, dt=f32):
            return ctx.enter_context(nc.sbuf_tensor(name, shape, dt))

        ident = sb("ident", [128, 128])
        ones = sb("ones", [1, 128])
        neg_half = sb("neg_half", [T, 8])
        pos = sb("pos", [T, 2, D])
        w_tok = sb("w_tok", [2 * CH * PS, PS // 2, D])
        w_in = {x: sb(f"w_in_{x}", [128, NPASS, 3 * D], f32r) for x in "ab"}
        w_out = {x: sb(f"w_out_{x}", [128, NPASS, D], f32r) for x in "ab"}
        w_fc1 = sb("w_fc1", [128, NPASS, HID], f32r)
        w_fc2 = sb("w_fc2", [128, HC, sum(KEEP_CH)])
        bias_qk = sb("bias_qk", [128, 3])
        bias_fc1 = sb("bias_fc1", [128, 3, HC])
        const_out = {x: sb(f"const_out_{x}", [T, D]) for x in "ab"}
        const_fc2 = sb("const_fc2", [T, D])
        gain = sb("gain", [128, 3])
        shift = sb("shift", [128, 3])
        v_bias = sb("v_bias", [128, 2])
        gum_row = sb("gum_row", [1, 3])
        gum_col = sb("gum_col", [3, 1])
        gum_all = sb("gum_all", [128, 3])
        fc1_raw = sb("fc1_raw", [128, HC])
        img = sb("img", [2 * CH * PS, IMW])
        xn = {x: sb(f"xn_{x}", [T, 4, D]) for x in "ab"}
        parts = {x: sb(f"parts_{x}", [128, 4 * 2 * D]) for x in "ab"}
        xT = {x: sb(f"xT_{x}", [128, 3, TP], f32r) for x in "ab"}
        qk_hi = {x: sb(f"qk_hi_{x}", [128, 3, TP]) for x in "ab"}
        q_st = {x: sb(f"q_st_{x}", [128, 6, TP], f32r) for x in "ab"}
        k_st = {x: sb(f"k_st_{x}", [128, 6, TP], f32r) for x in "ab"}
        vt = {x: sb(f"vt_{x}", [T, 4, HEADS, 32]) for x in "ab"}
        probs = sb("probs", [T, 4, 2, TP])
        h = sb("h", [T, 4, D])
        h2 = sb("h2", [T, 4, D])
        h2c = sb("h2c", [T, 4, D])
        y = sb("y", [T, 4, D])
        x2 = sb("x2", [T, 4, D])
        hid = sb("hid", [128, HT_SLOTS, TP])
        stats = {x: sb(f"stats_{x}", [T, 4, 6]) for x in "ab"}
        mv = {x: sb(f"mv_{x}", [T, 4, 2]) for x in "ab"}
        ve = {x: sb(f"ve_{x}", [T, 2, 4]) for x in "ab"}
        rstd = {x: sb(f"rstd_{x}", [T, 2, 4]) for x in "ab"}
        rden = {x: sb(f"rden_{x}", [T, 4, HEADS]) for x in "ab"}
        carrier = sb("carrier", [1, 1 + len(LEAD)])
        neg_max = sb("neg_max", [T, 4, HEADS])
        max_rows = sb("max_rows", [HEADS, TP], f32r)
        xs = {x: parts[x][0:T, :].rearrange("p (t n) -> p t n", t=4) for x in "ab"}
        qk_lo = {x: parts[x][:, 0:3 * TP].rearrange("p (c n) -> p c n", c=3) for x in "ab"}
        oT = qk_hi
        stage = hid[:, :, :].rearrange("p s n -> p (s n)")

        rows = hid[0:3, 7, 0:2 * D]
        bout_row = hid[0:1, 6, 0:D]
        b2_row = hid[0:1, 6, D:2 * D]
        one_row = hid[0:1, HT_SLOTS - 1, :]

        score_ps = ctx.enter_context(nc.psum_tensor("score_ps", [128, 4, 512], f32))
        bank = ctx.enter_context(nc.psum_tensor("bank", [128, 4, 512], f32))

        names = sorted({n for p in phases for n in p.end})
        sem = {n: ctx.enter_context(nc.semaphore(n)) for n in names}
        vec_chain = ctx.enter_context(nc.semaphore("vec_chain"))
        setup_in = ctx.enter_context(nc.semaphore("setup_in"))
        setup_sums = ctx.enter_context(nc.semaphore("setup_sums"))
        setup_done = ctx.enter_context(nc.semaphore("setup_done"))
        setup_link = ctx.enter_context(nc.semaphore("setup_link"))

        def slots(n):
            return stage[:, 0:3 * n].rearrange("p (s n) -> p s n", s=3)

        def raw(n, s):
            return stage[:, s * n:(s + 1) * n]

        def raw_hi(n):
            return stage[64:128, n:2 * n]

        B_TASKS = ["in_b", "out_b", "const_b", "fc1", "fc2"]
        TASKS = {0: ["tok", "in_a", "out_a", "const_a"], 1: [], 2: B_TASKS, 3: B_TASKS, 4: [], 5: []}

        def loads(k, task):
            set_ = "l" if k == LARGE_PHASE else "s"
            if task == "tok":
                return [(w_tok[:, :, :], I["w_tok"]), (pos[:, :, :], I["pos"]), (ident[:, :], I["ident"]),
                        (rows[0:2, 0:D], I["cls_b"]), (rows[0:2, D:D + D], I["tok_rows"][:, 0:D]),
                        (rden["a"][0:2, 0, 0:6], I["tok_rows"][:, D:TI])] + [
                            (k_st["b"][64 * e + 63:64 * e + 64, t, :].bitcast(f32), one_row) for e in range(2) for t in range(6)]
            if task == "in_a":
                return [(slots(3 * D), I["w_in_a"])]
            if task == "in_b":
                return [(slots(3 * D), I["w_in_b"]), (gain[:, :], I[f"n1{set_}_g"]), (shift[:, :], I[f"n1{set_}_b"])]
            if task == "out_a":
                return [(slots(D), I["w_out_a"]), (bout_row[:, :], I["b_out_a"])]
            if task == "out_b":
                more = [(rows[:, 0:D], I["keep_cols"]), (hid[0:3, 3, 0:3 * 128], I["keep_rows"]),
                        (gum_col[:, :], I["gum_col"])] if k == SMALL else []
                return [(slots(D), I["w_out_b"]), (bout_row[:, :], I["b_out_b"]), (b2_row[:, :], I["b_fc2"])] + more
            if task == "fc1":
                return [(slots(HID), I["w_fc1"]), (gain[:, :], I[f"n2{set_}_g"]), (shift[:, :], I[f"n2{set_}_b"]),
                        (fc1_raw[:, :], I["b_fc1"])]
            if task == "fc2":
                return [(stage[:, 0:HC * D].rearrange("p (m n) -> p m n", m=HC), I["w_fc2"])] + (
                    [(gum_row[:, :], I["gum_row"])] if k == SMALL else [])
            return []

        at_load, at_task, n_load, n_task = {}, {}, 0, 0
        for k in range(len(PHASES)):
            for task in TASKS[k]:
                n_load += 16 * len(loads(k, task))
                n_task += 1
                at_load[k, task], at_task[k, task] = n_load, n_task

        def setup_sync(sp, k):
            for task in TASKS[k]:
                if at_task[k, task] > 1:
                    sp.wait_ge(setup_done, at_task[k, task] - 1)
                for dst, src in loads(k, task):
                    sp.dma_start(dst, src).then_inc(setup_in, 16)

        def setup_tensor(pe, k):
            mm = nc.tensor.matmul
            for task in TASKS[k]:
                pe.wait_ge(setup_in, at_load[k, task])
                if at_task[k, task] > 1:
                    pe.wait_ge(setup_done, at_task[k, task] - 1)
                last = None
                if task == "tok":
                    pe.wait_ge(setup_link, 1)
                    mm(bank[0:T, 0, 0:D], rows[0:2, D:D + T], rows[0:2, 0:D], start=True, stop=True)
                    last = mm(bank[0:T, 0, D:2 * D], w_fc2[0:2, 0, 0:T], rows[0:2, 0:D], start=True, stop=True)
                if task == "in_b":
                    for c in range(3):
                        mm(bank[:, 1, c:c + 1], raw(576, 0)[:, c * 128:(c + 1) * 128], shift[:, 0:1], start=True, stop=False)
                        mm(bank[:, 1, c:c + 1], raw_hi(576)[:, c * 128:(c + 1) * 128], shift[64:128, 1:2], start=False, stop=True)
                    for c, n in ((0, 128), (1, 64)):
                        at = 2 * D + c * 128
                        mm(bank[128 - n:128, 2, c:c + 1], raw(576, 0)[:, at:at + n], shift[:, 0:1], start=True, stop=False)
                        last = mm(bank[128 - n:128, 2, c:c + 1], raw_hi(576)[:, at:at + n], shift[64:128, 1:2], start=False, stop=True)
                if task == "out_b" and k == SMALL:
                    pe.wait_ge(setup_link, link_at["cols"])
                    for s in range(3):
                        last = mm(bank[:, s, 0:D], hid[0:3, 3, s * 128:(s + 1) * 128], rows[0:3, 0:D], start=True, stop=True)
                if task in ("const_a", "const_b"):
                    last = mm(bank[0:T, 3, 0:D], ones[0:1, 0:T], bout_row[:, :], start=True, stop=task == "const_a")
                    if task == "const_b":
                        mm(bank[0:T, 3, 0:D], vbr(0), raw(D, 0), start=False, stop=False)
                        last = mm(bank[0:T, 3, 0:D], vbr(1), raw_hi(D), start=False, stop=True)
                if task == "fc1":
                    for n in range(phases[k].branches):
                        low = min(KEEP_CH[n], 128)
                        for m in range(HC):
                            at = bank[:, (0, 2, 3)[n], m:m + 1]
                            last = mm(at, stage[0:low, m * 128:(m + 1) * 128], shift[0:low, 0:1], start=True, stop=low < 128)
                            if low == 128:
                                last = mm(at, raw_hi(HID)[:, m * 128:(m + 1) * 128], shift[64:128, 1:2], start=False, stop=True)
                if task == "fc2":
                    last = mm(bank[0:T, 1, 0:D], ones[0:1, 0:T], b2_row[:, :], start=True, stop=True)
                    if k == SMALL:
                        last = mm(bank[:, 0, 0:3], ones[:, :], gum_row[:, :], start=True, stop=True)
                if last is not None:
                    last.then_inc(setup_sums, 1)

        def vbr(c):
            return stage[(0, 64)[c]:128, 3 * D + c * T:3 * D + (c + 1) * T]

        HAS_SUMS = {"tok", "in_b", "const_a", "const_b", "fc1", "fc2"}
        at_sums, n_sums = {}, 0
        for k in range(len(PHASES)):
            for task in TASKS[k]:
                n_sums += task in HAS_SUMS or (task == "out_b" and k == SMALL)
                at_sums[k, task] = n_sums
        link_at = {"cols": None}

        def setup_vector(v, k, links):
            def link(ins):
                links[0] += 1
                ins.then_inc(setup_link, 1)
                v.wait_ge(setup_link, links[0])

            def store(w, n):
                link(nc.vector.tensor_copy(w[:, 0:3, :], slots(n)))
                nc.vector.tensor_tensor(w[:, 3, :], raw(n, 0), w[:, 0, :].bitcast(f32), ALU.subtract)
                return nc.vector.tensor_tensor(w[64:128, 4, :], raw_hi(n), w[64:128, 1, :].bitcast(f32), ALU.subtract)

            for task in TASKS[k]:
                v.wait_ge(setup_in, at_load[k, task])
                if task == "tok":
                    link(tok_rows(v))
                if task == "out_b" and k == SMALL:
                    link(nc.vector.tensor_scalar(rows[:, 0:D], rows[:, 0:D], gum_col[:, 0:1], None, ALU.mult))
                if task in HAS_SUMS or (task == "out_b" and k == SMALL):
                    v.wait_ge(setup_sums, at_sums[k, task])
                if task == "tok":
                    last = nc.vector.tensor_tensor(pos[:, :, :], bank[0:T, 0, 0:2 * D].rearrange("p (u n) -> p u n", u=2),
                                                   pos[:, :, :], ALU.add)
                if task in ("in_a", "in_b"):
                    if task == "in_b":
                        nc.vector.tensor_scalar(bias_qk[0:64, :], bank[0:64, 1, 0:3], HD ** -0.5, None, ALU.mult)
                        nc.vector.tensor_copy(bias_qk[64:128, :], bank[64:128, 1, 0:3])
                        nc.vector.tensor_copy(v_bias[:, 0:1], bank[:, 2, 0:1])
                        nc.vector.tensor_copy(v_bias[64:128, 1:2], bank[64:128, 2, 1:2])
                        for s in range(3):
                            link(nc.vector.tensor_scalar(raw(576, s), raw(576, s), gain[:, s:s + 1], None, ALU.mult))
                    for s in range(3):
                        q = raw(576, s)[:, 0:2 * D].rearrange("p (c n) -> p c n", c=3)[:, :, 0:64]
                        link(nc.vector.tensor_scalar(q, q, HD ** -0.5, None, ALU.mult))
                    last = store(w_in[task[-1]], 3 * D)
                if task == "out_a":
                    last = store(w_out["a"], D)
                if task == "out_b":
                    if k == SMALL:
                        for s in range(3):
                            link(nc.vector.tensor_tensor(raw(D, s), bank[:, s, 0:D], raw(D, s), ALU.mult))
                        link(nc.vector.tensor_tensor(bout_row[:, :], bank[0:1, 0, 0:D], bout_row[:, :], ALU.mult))
                        link(nc.vector.tensor_tensor(b2_row[:, :], bank[0:1, 0, 0:D], b2_row[:, :], ALU.mult))
                    link(nc.vector.memset(stage[:, 3 * D:3 * D + 2 * T], 1.0))
                    for c in range(2):
                        link(nc.vector.tensor_scalar(vbr(c), vbr(c), v_bias[(0, 64)[c]:128, c:c + 1], None, ALU.mult))
                    last = store(w_out["b"], D)
                if task in ("const_a", "const_b"):
                    last = nc.vector.tensor_copy(const_out[task[-1]][:, :], bank[0:T, 3, 0:D])
                if task == "fc1":
                    for n in range(phases[k].branches):
                        nc.vector.tensor_tensor(bias_fc1[:, n, :], bank[:, (0, 2, 3)[n], 0:HC], fc1_raw[:, :], ALU.add)
                    for s in range(3):
                        link(nc.vector.tensor_scalar(raw(HID, s), raw(HID, s), gain[:, s:s + 1], None, ALU.mult))
                    last = store(w_fc1, HID)
                if task == "fc2":
                    src = stage[:, 0:HC * D].rearrange("p (m n) -> p m n", m=HC)
                    if k == LARGE_PHASE:
                        nc.vector.tensor_copy(w_fc2[:, :, 0:D], src)
                    else:
                        link(nc.vector.tensor_copy(gum_all[:, :], bank[:, 0, 0:3]))
                        at = 0
                        for n in range(3):
                            nc.vector.tensor_scalar(w_fc2[:, :, at:at + KEEP_CH[n]], src[:, :, 0:KEEP_CH[n]],
                                                    gum_all[:, n:n + 1], None, ALU.mult)
                            at += KEEP_CH[n]
                    last = nc.vector.tensor_copy(const_fc2[:, :], bank[0:T, 1, 0:D])
                last.then_inc(setup_done, 1)

        def tok_rows(v):
            nc.vector.tensor_copy(w_fc2[0:2, 0, 0:D - T], rows[0:2, D + T:2 * D])
            return nc.vector.tensor_copy(w_fc2[0:2, 0, D - T:T], rden["a"][0:2, 0, 0:6])

        def count_links():
            n = 0
            for k in range(len(PHASES)):
                for task in TASKS[k]:
                    if task == "tok":
                        n += 1
                    if task == "out_b" and k == SMALL:
                        link_at["cols"] = n + 1
                        n += 1 + 5
                    if task == "in_a":
                        n += 3 + 1
                    if task == "in_b":
                        n += 3 + 3 + 1
                    if task == "out_a":
                        n += 1
                    if task == "out_b":
                        n += 1 + 2 + 1
                    if task == "fc1":
                        n += 3 + 1
                    if task == "fc2" and k == SMALL:
                        n += 1
        count_links()

        def tile_mm(dst, lhs, rhs, first, last):
            return nc.tensor.matmul(dst, lhs, rhs, start=first, stop=last)

        def by_feature(dst, x, w, col, width, n0=0, n=TP):
            ps = passes(width)
            for j, (c, r0, r1, s) in enumerate(ps):
                ins = tile_mm(dst, w[r0:r1, s, col:col + 128], xT[x][r0:r1, c, n0:n0 + n], j == 0, j == len(ps) - 1)
            return ins

        def by_token(dst, x, tt, w, col, n):
            ps = passes(D)
            for j, (c, r0, r1, s) in enumerate(ps):
                ins = tile_mm(dst, xT[x][r0:r1, c, tt * T:(tt + 1) * T], w[r0:r1, s, col:col + n], j == 0, j == len(ps) - 1)
            return ins

        def unit(n):
            g, i, hp = n // 4, (n // 2) % 2, n % 2
            return g, i, hp, 2 * g + hp

        def sync_step(sp, ph, step, it):
            x, what, n = step
            if what == "img":
                b = 2 * (it + 2) + n if ph.count == 1 else sp.snap(2 * (it + 2) + n)
                made = ph.ahead("tok_made", step, it)
                if made is not None:
                    sp.wait_ge(sem["tok_made"], made)
                for g in range(2):
                    for c in range(CH):
                        p = (g * CH + c) * PS
                        at = PS - g * (PS // 2)
                        sp.dma_start(img[p:p + PS, at:at + NP * IMG].rearrange("p (py w) -> p py w", w=IMG),
                                     I["x"][b, c].rearrange("(py ph) w -> ph py w", ph=PS)).then_inc(sem["img_in"], 16)
            if what == "stack":
                last = (x, "qk", 2)
                sp.wait_ge(sem[f"bank_read{ph.turn[last]}"], ph.upto(f"bank_read{ph.turn[last]}", last, it))
                v = ph.ahead("pv_done", step, it)
                if v is not None:
                    sp.wait_ge(sem["pv_done"], v)
                for side, dst, kinds in ((0, q_st, "hhl"), (1, k_st, "hlh")):
                    for g, kind in enumerate(kinds):
                        src = qk_hi[x] if kind == "h" else qk_lo[x]
                        for b2 in range(2):
                            r = 64 * side + 32 * b2
                            sp.dma_start(dst[x][g:128:4, 3 * b2:3 * b2 + 3, :].bitcast(f32), src[r:r + 32, :, :])\
                                .then_inc(sem[f"stack_in_{x}"], 16)
            if what == "mrow":
                t = ph.turn[step]
                sp.wait_ge(sem[f"bank_read{t}"], ph.upto(f"bank_read{t}", step, it))
                for e in range(2):
                    sp.dma_start(q_st["b"][64 * e + 63:64 * e + 64, :, :].bitcast(f32),
                                 max_rows[6 * e:6 * e + 6, :].bitcast(f32)).then_inc(sem["mrow_in"], 16)

        def tensor_step(pe, ph, step, it):
            x, what, n = step
            t = ph.turn.get(step)

            def bank_free():
                v = ph.ahead(f"bank_read{t}", step, it)
                if v is not None:
                    pe.wait_ge(sem[f"bank_read{t}"], v)

            if what == "tok":
                bank_free()
                pe.wait_ge(sem["img_in"], ph.upto("img_in", ("a", "img", n), it))
                for u in range(2):
                    for j in range(PS // 2):
                        at = u * (T - 1) * PS + u * PS + j
                        ins = tile_mm(bank[0:T, t, u * D:(u + 1) * D], img[:, at:at + (T - 1) * PS + 1:PS],
                                      w_tok[:, j, :], j == 0, j == PS // 2 - 1)
                ins.then_inc(sem["tok_made"], 1)
            if what == "xT":
                bank_free()
                s = (x, "split", n // 3)
                pe.wait_ge(sem[f"split_done_{x}"], ph.seen(f"split_done_{x}", s, step, it))
                c = n % 3
                for tt in range(4):
                    ins = nc.tensor.transpose(bank[:, t, tt * T:(tt + 1) * T], xs[x][:, tt, c * 128:(c + 1) * 128], ident[0:T, 0:T])
                ins.then_inc(sem[f"bank_full{t}"], 1)
            if what in ("qk", "v", "proj", "fc1"):
                bank_free()
                which = {"qk": 0, "v": 0, "proj": 1, "fc1": 2}[what]
                wait_read(pe, ph, [(x, "xT", 3 * which + c) for c in range(3)], it, t)
                if what == "qk":
                    ins = by_feature(bank[:, t, 0:TP], x, w_in[x], n * 128, D)
                if what == "fc1":
                    ins = by_feature(bank[:, t, 0:TP], x, w_fc1, n % HC * 128, KEEP_CH[n // HC])
                if what in ("v", "proj"):
                    w, col = (w_in[x], 2 * D) if what == "v" else (w_out[x], 0)
                    for u in range(2):
                        ins = by_token(bank[0:T, t, u * D:(u + 1) * D], x, 2 * n + u, w, col, D)
                ins.then_inc(sem[f"bank_full{t}"], 1)
            if what in SCORE_STEPS:
                v = ph.ahead(f"score_read{t}", step, it)
                if v is not None:
                    pe.wait_ge(sem[f"score_read{t}"], v)
                pe.wait_ge(sem[f"stack_in_{x}"], ph.upto(f"stack_in_{x}", (x, "stack", 0), it))
                if what == "score" and x == "b":
                    pe.wait_ge(sem["mrow_in"], ph.upto("mrow_in", ("b", "mrow", 0), it))
                g, i, hp, tile = unit(n)
                rows_ = 64 if what == "score" else 63
                left, right = (k_st, q_st) if what == "score" else (q_st, k_st)
                for u in range(2):
                    for e in range(2):
                        r = slice(64 * e, 64 * e + rows_)
                        ins = tile_mm(score_ps[0:T, 2 * t + e, u * TI:(u + 1) * TI],
                                      left[x][r, tile, i * TI + u * T:i * TI + (u + 1) * T],
                                      right[x][r, tile, i * TI:(i + 1) * TI], True, True)
                ins.then_inc(sem[f"score_full{t}"], 1)
            if what == "pv":
                g, i = n // 2, n % 2
                if i == 0:
                    bank_free()
                for s, st in {ph.turn[st]: st for st in ((x, "score", 2 * n), (x, "score", 2 * n + 1))}.items():
                    pe.wait_ge(sem[f"score_read{s}"], ph.upto(f"score_read{s}", st, it))
                wait_read(pe, ph, [(x, "v", i)], it, t if i == 0 else None)
                for u in range(2):
                    keys = T - u
                    for hp in range(2):
                        for e in range(2):
                            qd = 2 * hp + e
                            ins = tile_mm(bank[32 * qd:32 * qd + 32, t, i * TI:(i + 1) * TI],
                                          vt[x][0:keys, 2 * i + u, 4 * g + qd, :],
                                          probs[0:keys, ph.weights.index((x, "score", 2 * n + hp)) % 4, e, u * TI:(u + 1) * TI],
                                          u == 0, u == 1)
                ins.then_inc(sem["pv_done"], 1)
            if what == "back":
                bank_free()
                wait_read(pe, ph, [(x, "ot", 2)], it, t)
                for g in range(3):
                    ins = nc.tensor.transpose(bank[0:T, t, g * 128:(g + 1) * 128], oT[x][:, g, n * T:(n + 1) * T], ident[:, :])
                ins.then_inc(sem[f"bank_full{t}"], 1)
            if what == "mrow":
                bank_free()
                st = ("b", "max", 11)
                pe.wait_ge(sem[f"score_read{ph.turn[st]}"], ph.upto(f"score_read{ph.turn[st]}", st, it))
                for tt in range(4):
                    ins = nc.tensor.transpose(bank[0:HEADS, t, tt * T:(tt + 1) * T], neg_max[:, tt, :], ident[0:T, 0:T])
                ins.then_inc(sem[f"bank_full{t}"], 1)
            if what == "fc2":
                bank_free()
                br, i = n // 2, n % 2
                wait_read(pe, ph, [("b", "fc1", br * HC + m) for m in range(HC)], it, t)
                width, at = KEEP_CH[br], sum(KEEP_CH[:br])
                for u in range(2):
                    tt = 2 * i + u
                    for m in range(HC):
                        ins = tile_mm(bank[0:T, t, u * D:u * D + width], hid[:, (br * HC + m) % HT_SLOTS, tt * T:(tt + 1) * T],
                                      w_fc2[:, m, at:at + width], m == 0, m == HC - 1)
                ins.then_inc(sem[f"bank_full{t}"], 1)

        def full(eng, ph, step, it):
            t = ph.turn[step]
            eng.wait_ge(sem[f"bank_full{t}"], ph.upto(f"bank_full{t}", step, it))
            return t

        def scalar_step(act, ph, step, it):
            x, what, n = step
            if (x, what, n) == ("b", "norm", 0):
                wait_read(act, ph, [("a", "proj", i) for i in range(2)], it)
                val = ph.ahead("f_half", step, it)
                if val is not None:
                    act.wait_ge(sem["f_half"], val)
                nc.scalar.activation(h2c[:, :, :], h2[:, :, :], ACT.Identity).then_inc(sem["hc_ready"], 1)
            if what == "split":
                wait_xn(act, ph, step, it)
                if n == 1:
                    act.wait_ge(sem[f"stack_in_{x}"], ph.upto(f"stack_in_{x}", (x, "stack", 0), it))
                else:
                    st = (x, "xT", 5 if n == 2 or x == "a" else 8)
                    if st in ph.pos:
                        act.wait_ge(sem[f"bank_full{ph.turn[st]}"], ph.upto(f"bank_full{ph.turn[st]}", st, it))
                nc.scalar.activation(xs[x][:, :, 0:128].bitcast(f32r), xn[x][:, :, 0:128], ACT.Identity)
                nc.scalar.activation(xs[x][:, :, 192:256].bitcast(f32r), xn[x][:, :, 128:D], ACT.Identity)\
                    .then_inc(sem["hi_ready"], 1)
            if what == "xT" and n % 3 != 1:
                t = full(act, ph, step, it)
                nc.scalar.activation(xT[x][:, n % 3, :], bank[:, t, 0:TP], ACT.Identity).then_inc(sem[f"bank_read{t}"], 1)
            if what == "qk":
                t = full(act, ph, step, it)
                bias = bias_qk[:, n:n + 1] if x == "b" else 0.0
                nc.scalar.activation(qk_hi[x][:, n, :].bitcast(f32r), bank[:, t, 0:TP], ACT.Identity, bias=bias)\
                    .then_inc(sem["qk_hi_ready"], 1)
            if what == "v":
                t = full(act, ph, step, it)
                nc.scalar.activation(vt[x][:, 2 * n:2 * n + 2, :, 0:HD],
                                     bank[0:T, t, 0:2 * D].rearrange("p (u h d) -> p u h d", u=2, h=HEADS),
                                     ACT.Identity).then_inc(sem[f"bank_read{t}"], 1)
            if what == "score":
                t = ph.turn[step]
                act.wait_ge(sem[f"score_full{t}"], ph.upto(f"score_full{t}", step, it))
                w = ph.weights.index(step)
                if w >= 4:
                    x4, _, n4 = ph.weights[w - 4]
                    v = ph.upto("pv_done", (x4, "pv", n4 // 2), it)
                else:
                    v = ph.ahead("pv_done", step, it)
                if v is not None:
                    act.wait_ge(sem["pv_done"], v)
                func, bias = (ACT.Square, 1.0) if x == "a" else (ACT.Exp, 0.0)
                nc.scalar.activation(probs[:, w % 4, :, :], score_ps[0:T, 2 * t:2 * t + 2, 0:TP], func, bias=bias)\
                    .then_inc(sem[f"score_read{t}"], 1)
            if what == "mrow":
                t = full(act, ph, step, it)
                nc.scalar.activation(max_rows[:, :], bank[0:HEADS, t, 0:TP], ACT.Identity).then_inc(sem[f"bank_read{t}"], 1)
            if what == "fc1":
                t = full(act, ph, step, it)
                if n >= HT_SLOTS:
                    for i in range(2):
                        st = ("b", "fc2", 2 * ((n - HT_SLOTS) // HC) + i)
                        if ph.turn[st] != t:
                            act.wait_ge(sem[f"bank_full{ph.turn[st]}"], ph.upto(f"bank_full{ph.turn[st]}", st, it))
                nc.scalar.activation(hid[:, n % HT_SLOTS, :], bank[:, t, 0:TP], ACT.Gelu,
                                     bias=bias_fc1[:, n // HC, n % HC:n % HC + 1]).then_inc(sem[f"bank_read{t}"], 1)
            if what == "out":
                for i in range(2):
                    st = ("b", "fc2", 2 * ph.branches - 2 + i)
                    act.wait_ge(sem[f"bank_read{ph.turn[st]}"], ph.upto(f"bank_read{ph.turn[st]}", st, it))
                for i in range(2):
                    for u in range(2):
                        act.dma_start(out[2 * it + i, u * T:u * T + T - u, :], x2[0:T - u, 2 * i + u, :])\
                            .then_inc(sem["out_done"], 16)

        def wait_xn(eng, ph, step, it):
            x, _, n = step
            if n == 1:
                st = (x, "back", 3)
                t = ph.turn[st]
                eng.wait_ge(sem[f"bank_read{t}"], ph.upto(f"bank_read{t}", st, it))
            else:
                eng.wait_ge(sem["xn_ready"], ph.upto("xn_ready", (x, "norm", n // 2), it))

        def pool_step(pool, ph, step, it):
            x, what, n = step
            if what == "norm":
                pool.wait_ge(sem["var_ready"], ph.upto("var_ready", step, it))
                nc.gpsimd.tensor_tensor(rstd[x][:, :, :], ve[x][:, :, :], neg_half[:, :].rearrange("p (a b) -> p a b", a=2),
                                        ALU.pow).then_inc(sem["rstd_ready"], 1)
                if x == "a":
                    pool.wait_ge(sem["xn_ready"], ph.upto("xn_ready", step, it))
                    val = ph.ahead("hc_ready", step, it)
                    if val is not None:
                        pool.wait_ge(sem["hc_ready"], val)
                    nc.gpsimd.tensor_tensor(h2[:, :, :], h[:, :, :], const_out["a"][:, :].unsqueeze(1).to_broadcast([T, 4, D]),
                                            ALU.add).then_inc(sem["hb_ready"], 1)
            if what == "const":
                pool.wait_ge(sem["y_ready"], ph.seen("y_ready", ("b", "norm", 0), step, it))
                nc.gpsimd.tensor_tensor(y[:, :, :], y[:, :, :], const_out["b"][:, :].unsqueeze(1).to_broadcast([T, 4, D]),
                                        ALU.add).then_inc(sem["yb_ready"], 1)
            if what == "sum":
                pool.wait_ge(sem["xn_ready"], ph.upto("xn_ready", ("b", "norm", 1), it))
                pool.wait_ge(sem["hc_ready"], ph.seen("hc_ready", ("b", "norm", 0), step, it))
                nc.gpsimd.tensor_tensor(x2[:, :, :], x2[:, :, :], h2c[:, :, :], ALU.add).then_inc(sem["f_half"], 1)
                pool.wait_ge(sem["f_half"], ph.upto("f_half", step, it))
                nc.gpsimd.tensor_tensor(x2[:, :, :], x2[:, :, :], const_fc2[:, :].unsqueeze(1).to_broadcast([T, 4, D]),
                                        ALU.add).then_inc(sem["f_ready"], 1)
            if what == "split":
                pool.wait_ge(sem["hi_ready"], ph.upto("hi_ready", step, it))
                nc.gpsimd.tensor_tensor(xs[x][:, :, 128:192].bitcast(f32r), xn[x][:, :, 0:64], xs[x][:, :, 0:64], ALU.subtract)\
                    .then_inc(sem[f"split_done_{x}"], 1)
                nc.gpsimd.tensor_tensor(xs[x][:, :, 256:320].bitcast(f32r), xn[x][:, :, 64:128], xs[x][:, :, 64:128], ALU.subtract)\
                    .then_inc(sem[f"split_done_{x}"], 1)
                nc.gpsimd.tensor_tensor(xs[x][:, :, 320:384].bitcast(f32r), xn[x][:, :, 128:D], xs[x][:, :, 192:256], ALU.subtract)\
                    .then_inc(sem[f"split_done_{x}"], 1)

        def vector_step(v, ph, step, it):
            x, what, n = step
            if what == "tok":
                t = ph.turn[step]
                v.wait_ge(sem["tok_made"], ph.upto("tok_made", step, it))
                val = ph.ahead("hb_ready", step, it)
                if val is not None:
                    v.wait_ge(sem["hb_ready"], val)
                nc.vector.tensor_tensor(h[:, 2 * n:2 * n + 2, :], bank[0:T, t, 0:2 * D].rearrange("p (u n) -> p u n", u=2),
                                        pos[:, :, :], ALU.add).then_inc(sem[f"bank_read{t}"], 1)
            if what == "norm":
                src = {("a", 0): h, ("b", 0): h2, ("b", 1): x2}[x, n]
                if (x, n) == ("a", 0):
                    wait_read(v, ph, [("a", "tok", i) for i in range(2)], it)
                if (x, n) == ("b", 0):
                    wait_read(v, ph, [("a", "proj", i) for i in range(2)], it)
                if (x, n) == ("b", 1):
                    wait_read(v, ph, [("b", "proj", i) for i in range(2)], it)
                for tt in range(4):
                    ins = nc.vector.bn_stats(stats[x][:, tt, :], src[:, tt, :])
                ins.then_inc(sem["stats_ready"], 1)
                v.wait_ge(sem["stats_ready"], ph.upto("stats_ready", step, it, 1))
                nc.vector.memset(carrier[:, 0:1], 0.0)
                for tt in range(4):
                    ins = nc.vector.bn_aggr(mv[x][:, tt, :], stats[x][:, tt, :])
                ins.then_inc(sem["stats_ready"], 1)
                v.wait_ge(sem["stats_ready"], ph.upto("stats_ready", step, it, 2))
                var = mv[x][:, :, 1]
                nc.vector.tensor_scalar(ve[x][:, 0, :], var, EPS, None, ALU.add)
                two = (1.0 + EPS, EPS * EPS) if (x, n) == ("b", 0) else (1.0, EPS)
                nc.vector.tensor_scalar(ve[x][:, 1, :], var, two[0], two[1], ALU.mult, ALU.add).then_inc(sem["var_ready"], 1)
                v.wait_ge(sem["rstd_ready"], ph.upto("rstd_ready", step, it))
                read_xn(v, ph, step, it)
                for tt in range(4):
                    ins = nc.vector.tensor_scalar(xn[x][:, tt, :], src[:, tt, :], mv[x][:, tt, 0:1], rstd[x][:, 1, tt:tt + 1],
                                                  ALU.subtract, ALU.mult)
                ins.then_inc(sem["xn_ready"], 1)
                if (x, n) == ("b", 0):
                    for tt in range(4):
                        ins = nc.vector.tensor_scalar(y[:, tt, :], src[:, tt, :], mv[x][:, tt, 0:1], rstd[x][:, 0, tt:tt + 1],
                                                      ALU.subtract, ALU.mult)
                    ins.then_inc(sem["y_ready"], 1)
            if what == "xT" and n % 3 == 1:
                t = full(v, ph, step, it)
                nc.vector.tensor_copy(xT[x][:, 1, :], bank[:, t, 0:TP]).then_inc(sem[f"bank_read{t}"], 1)
            if what == "qk":
                t = ph.turn[step]
                v.wait_ge(sem["qk_hi_ready"], ph.upto("qk_hi_ready", step, it))
                bias = bias_qk[:, n:n + 1] if x == "b" else 0.0
                nc.vector.scalar_tensor_tensor(qk_lo[x][:, n, :].bitcast(f32r), bank[:, t, 0:TP], bias, qk_hi[x][:, n, :],
                                               ALU.add, ALU.subtract).then_inc(sem[f"bank_read{t}"], 1)
            if what == "max":
                t = ph.turn[step]
                g, i, hp, tile = unit(n)
                v.wait_ge(sem[f"score_full{t}"], ph.upto(f"score_full{t}", step, it))
                dst = neg_max[:, 2 * i:2 * i + 2, :].rearrange("p u (e t) -> p e u t", e=2)[:, :, :, tile]
                src = score_ps[0:T, 2 * t:2 * t + 2, 0:TP].rearrange("p e (u k) -> p e u k", u=2)[:, :, :, 0:NTOK]
                nc.vector.tensor_reduce(dst, src, AX.X, ALU.max, negate=True).then_inc(sem[f"score_read{t}"], 1)
            if what == "ot":
                t = ph.turn[step]
                v.wait_ge(sem["pv_done"], ph.upto("pv_done", (x, "pv", 2 * n + 1), it))
                if x == "a":
                    for i in range(2):
                        ins = nc.vector.tensor_scalar(oT[x][:, n, i * TI:(i + 1) * TI], bank[:, t, i * TI:(i + 1) * TI],
                                                      bank[:, t, (i + 1) * TI - 1:(i + 1) * TI], None, ALU.add)
                else:
                    ins = nc.vector.tensor_copy(oT[x][:, n, :], bank[:, t, 0:TP])
                ins.then_inc(sem[f"bank_read{t}"], 1)
            if what == "back":
                t = full(v, ph, step, it)
                if n == 0:
                    read_xn(v, ph, step, it)
                o = bank[0:T, t, 0:3 * 128].rearrange("p (h d) -> p h d", h=HEADS)
                nc.vector.reciprocal(rden[x][:, n, :], o[:, :, HD]).then_inc(sem["rden_ready"], 1)
                v.wait_ge(sem["rden_ready"], ph.upto("rden_ready", step, it))
                nc.vector.tensor_tensor(xn[x][:, n, :].rearrange("p (h d) -> p h d", h=HEADS), o[:, :, 0:HD],
                                        rden[x][:, n, :].unsqueeze(2).to_broadcast([T, HEADS, HD]), ALU.mult)\
                    .then_inc(sem[f"bank_read{t}"], 1)
            if what == "proj":
                t = full(v, ph, step, it)
                if x == "a":
                    v.wait_ge(sem["hb_ready"], ph.seen("hb_ready", ("a", "norm", 0), step, it))
                    dst = src = h2
                else:
                    v.wait_ge(sem["yb_ready"], ph.upto("yb_ready", ("b", "const", 0), it))
                    val = ph.ahead("out_done", step, it)
                    if val is not None:
                        v.wait_ge(sem["out_done"], val)
                    dst, src = x2, y
                nc.vector.tensor_tensor(dst[:, 2 * n:2 * n + 2, :], bank[0:T, t, 0:2 * D].rearrange("p (u n) -> p u n", u=2),
                                        src[:, 2 * n:2 * n + 2, :], ALU.add).then_inc(sem[f"bank_read{t}"], 1)
            if what == "fc2":
                t = full(v, ph, step, it)
                br, i = n // 2, n % 2
                v.wait_ge(sem["f_ready"], ph.upto("f_ready", ("b", "sum", 0), it))
                if br:
                    wait_read(v, ph, [("b", "fc2", n - 2)], it)
                w = KEEP_CH[br]
                acc = x2[:, 2 * i:2 * i + 2, 0:w]
                nc.vector.tensor_tensor(acc, bank[0:T, t, 0:2 * D].rearrange("p (u n) -> p u n", u=2)[:, :, 0:w],
                                        acc, ALU.add).then_inc(sem[f"bank_read{t}"], 1)

        def read_xn(eng, ph, step, it):
            val = ph.ahead(f"split_done_{step[0]}", step, it)
            if val is not None:
                eng.wait_ge(sem[f"split_done_{step[0]}"], val)

        def wait_read(eng, ph, steps, it, free=None):
            for t, st in {ph.turn[st]: st for st in steps}.items():
                if t != free:
                    eng.wait_ge(sem[f"bank_read{t}"], ph.upto(f"bank_read{t}", st, it))

        def run(eng, ph, do):
            if ph.count > 1:
                with eng.Fori(ph.first, ph.first + ph.count) as it:
                    for step in ph.steps:
                        do(eng, ph, step, it)
            else:
                for step in ph.steps:
                    do(eng, ph, step, ph.first)

        links = [0]
        init = ctx.enter_context(nc.semaphore("init"))
        for k, ph in enumerate(phases):
            with nc.Block() as block:
                @block.sync
                def _(sp):
                    if k == 0:
                        sp.wait_ge(init, 10)
                    setup_sync(sp, k)
                    run(sp, ph, sync_step)

                @block.gpsimd
                def _(pool):
                    if k == 0:
                        nc.gpsimd.memset(neg_half[:, :], -0.5).then_inc(init, 1)
                        nc.gpsimd.memset(vt["a"][:, :, :, :], 1.0).then_inc(init, 1)
                        nc.gpsimd.memset(vt["b"][:, :, :, :], 1.0).then_inc(init, 1)
                        nc.gpsimd.memset(img[:, :], 0.0).then_inc(init, 1)
                        for st in (q_st["b"], k_st["b"]):
                            nc.gpsimd.memset(st[:, :, :].bitcast(f32), 0.0).then_inc(init, 1)
                        nc.gpsimd.memset(one_row, 1.0).then_inc(init, 1)
                        pool.wait_ge(init, 10)
                    if TASKS[k]:
                        pool.wait_ge(setup_done, at_task[k, TASKS[k][-1]])
                    run(pool, ph, pool_step)

                @block.vector
                def _(v):
                    if k == 0:
                        nc.vector.memset(ones[:, :], 1.0).then_inc(init, 1)
                        for st in (q_st["a"], k_st["a"]):
                            nc.vector.memset(st[:, :, :].bitcast(f32), 0.0).then_inc(init, 1)
                        for at, (name, lead) in enumerate(LEAD.items()):
                            nc.vector.memset(carrier[:, 1 + at:2 + at], 0.0).then_inc(sem[name], lead)
                    setup_vector(v, k, links)
                    run(v, ph, vector_step)

                @block.scalar
                def _(act):
                    if k == 0:
                        act.wait_ge(init, 10)
                    if TASKS[k]:
                        act.wait_ge(setup_done, at_task[k, TASKS[k][-1]])
                    run(act, ph, scalar_step)
                    if k == len(phases) - 1:
                        act.wait_ge(sem["out_done"], ph.end["out_done"])

                @block.tensor
                def _(pe):
                    if k == 0:
                        pe.wait_ge(init, 10)
                    setup_tensor(pe, k)
                    if TASKS[k]:
                        pe.wait_ge(setup_done, at_task[k, TASKS[k][-1]])
                    run(pe, ph, tensor_step)


def kernel(**inputs):
    import concourse.bacc as bacc
    from concourse.bass_utils import run_bass_kernel_spmd

    def get(name):
        return np.asarray(inputs[name])

    def stack(w):
        w = w.reshape(D, -1)
        return np.ascontiguousarray(np.stack([w[0:128], np.concatenate([w[0:64], w[128:192]]), w[64:192]], 1))

    cols = [side * D + (2 * (b2 * 3 + c) + e) * HD + d
            for c in range(3) for side in range(2) for b2 in range(2) for e in range(2) for d in range(HD)]
    cols += list(range(2 * D, 3 * D))
    f = np.float32
    pos = np.zeros((TI, D), f)
    pos[:NTOK] = get("L0_tok_pos_embed")
    tok_rows = np.zeros((2, TI), f)
    tok_rows[0, 0] = 1.0
    tok_rows[1, 1:NTOK] = 1.0
    w_tok = get("L0_tok_W").reshape(D, CH, PS, 2, PS // 2).transpose(3, 1, 2, 4, 0).reshape(2 * CH * PS, PS // 2, D)
    keep_rows = np.zeros((3, 3, 128), f)
    row_of = stack(np.arange(D))[:, :, 0].T
    for n in range(3):
        keep_rows[n] = row_of < KEEP_HEADS[n] * HD
    keep_cols = np.array([[c < KEEP_CH[n] for c in range(D)] for n in range(3)], f)
    gum = get("L0_ffn_gumbel_weights")
    arrays = {
        "x": get("x"), "w_tok": w_tok, "pos": pos.reshape(2, T, D).transpose(1, 0, 2), "ident": np.eye(128, dtype=f),
        "cls_b": np.stack([get("L0_tok_class_token")[0], get("L0_tok_b")]), "tok_rows": tok_rows,
        "w_in_a": stack(get("L0_attn_w_qkv")[:, cols]), "w_out_a": stack(get("L0_attn_w_proj")),
        "b_out_a": get("L0_attn_b_proj")[None],
        "w_in_b": stack(get("L0_ffn_w_qkv")[:, cols]), "w_out_b": stack(get("L0_ffn_w_proj")),
        "b_out_b": get("L0_ffn_b_proj")[None],
        "w_fc1": stack(get("L0_ffn_w_fc1")), "b_fc1": get("L0_ffn_b_fc1").reshape(HC, 128).T,
        "w_fc2": get("L0_ffn_w_fc2").reshape(HC, 128, D).transpose(1, 0, 2), "b_fc2": get("L0_ffn_b_fc2")[None],
        "keep_rows": keep_rows.reshape(3, 3 * 128), "keep_cols": keep_cols,
        "gum_col": gum[:, None], "gum_row": gum[None],
    }
    for name in ("n1l", "n1s", "n2l", "n2s"):
        for part in "gb":
            arrays[f"{name}_{part}"] = stack(get(f"L0_ffn_{name}_{part}"))[:, :, 0]
    arrays = {k: np.ascontiguousarray(v) for k, v in arrays.items()}
    nc = bacc.Bacc("TRN2", target_bir_lowering=False, num_devices=1)
    given = {k: nc.dram_tensor(f"in_{k}", v.shape, mybir.dt.from_np(v.dtype), kind="ExternalInput").ap()
             for k, v in arrays.items()}
    out = nc.dram_tensor("out", (B, NTOK, D), mybir.dt.float32, kind="ExternalOutput").ap()
    build(nc, given, out)
    r = run_bass_kernel_spmd(nc, [{f"in_{k}": v for k, v in arrays.items()}], core_ids=[0])
    return r.results[0]["out"]
```

```python
import concourse.bass as bass
from concourse import mybir
from contextlib import ExitStack
import numpy as np

B, NTOK, D = 64, 197, 192
HEADS, HD = 12, 16
HID = 4 * D
NP, PS, CH, IMG = 14, 16, 3, 224
T = 99
TI = 2 * T
TP = 2 * TI
PAIRS = B // 2
LARGE = PAIRS // 2
HC = HID // 128
NPASS = 5
KEEP_CH = [D, D // 2, D // 3]
KEEP_HEADS = [HEADS, HEADS // 2, HEADS // 3]
IMW = 2 * PS + IMG * NP
EPS = 1e-5
SCORE_TURNS, TURNS = 3, 5
NEAR = 2
HT_SLOTS = 9


def attention(x, lag):
    steps = []
    for k in range(12 + lag - 1):
        if k < 12:
            steps.append((x, "score", k))
        n = (k - lag) // 2
        if k >= lag and (k - lag) % 2 == 0:
            steps.append((x, "pv", n))
            if n % 2 == 1:
                steps.append((x, "ot", n // 2))
    return steps


def transposes(x, n):
    return [(x, "xT", 3 * n + c) for c in range(3)]


def project_in(x):
    return transposes(x, 0) + [(x, "qk", c) for c in range(3)] + [(x, "stack", 0), (x, "v", 0), (x, "v", 1)]


def back(x):
    return [(x, "back", t) for t in range(4)]


def merge(a, b):
    out, j = [], 0
    for i, s in enumerate(a):
        out.append(s)
        while j < len(b) and (j + 1) * len(a) <= (i + 1) * len(b):
            out.append(b[j])
            j += 1
    return out + b[j:]


def mlp(branches):
    fc1 = [("b", "fc1", m) for m in range(branches * HC)]
    steps = fc1[:HC]
    for n in range(branches):
        half = (n + 1) * HC + HC // 2
        steps += fc1[(n + 1) * HC:half] + [("b", "fc2", 2 * n), ("b", "fc2", 2 * n + 1)] + fc1[half:half + HC // 2]
    return steps


def body(branches):
    att_a, att_b, maxes, fc = attention("a", 3), attention("b", 3), [("b", "max", k) for k in range(12)], mlp(branches)

    toks, in_a, in_b = [("a", "tok", n) for n in range(4)], project_in("a"), project_in("b")
    group = att_b.index(("b", "ot", 0)) + 1
    return (
        [("a", "img", 0), ("b", "const", 0)] + in_b + att_a[:3] + toks[:1] + att_a[3:8] + toks[1:2] + [("a", "img", 1)]
        + att_a[8:9] + maxes[:2] + merge([att_a[9], att_a[11], att_a[10]] + att_a[12:-4], maxes[2:]) + att_a[-4:-2] + [("b", "mrow", 0)] + att_a[-2:]
        + toks[2:3] + att_b[:3] + back("a") + [("a", "split", 1), ("a", "stats", 0)]
        + att_b[3:6] + toks[3:] + [("a", "stats", 1)] + att_b[6:group]
        + transposes("a", 1) + [("a", "norm", 0), ("a", "proj", 0), ("a", "proj", 1)]
        + att_b[group:group + 3] + [("a", "split", 0)] + att_b[group + 3:]
        + transposes("a", 0) + back("b") + [("b", "split", 1)] + in_a[3:4] + transposes("b", 1)
        + [("b", "proj", 0), ("b", "stats", 2), ("b", "proj", 1), ("b", "stats", 3), ("b", "norm", 1)] + in_a[4:]
        + [("b", "split", 2), ("b", "sum", 0)] + transposes("b", 2)
        + fc[:1] + [("b", "stats", 0), ("b", "stats", 1)] + fc[1:3] + [("b", "norm", 0)] + fc[3:5]
        + [("b", "split", 0), ("a", "residual", 0)] + fc[5:] + [("b", "out", 0)])


A_HEAD = [("a", "img", 0), ("a", "img", 1)] + [("a", "tok", n) for n in range(4)] + [
    ("a", "stats", 0), ("a", "stats", 1), ("a", "norm", 0), ("a", "split", 0), ("a", "residual", 0)] + project_in("a")
B_NEXT = [("b", "stats", 0), ("b", "stats", 1), ("b", "norm", 0), ("b", "split", 0)]


def order(kind, branches):
    steps = body(branches)
    if kind == "first":
        return [s for s in steps if s in A_HEAD]
    if kind == "a":
        return [s for s in steps if s[0] == "a" or s in B_NEXT]
    if kind == "b":
        return [s for s in steps if s[0] == "b" and s not in B_NEXT]
    if kind == "last":
        return [s for s in steps if s not in A_HEAD]
    return steps


PHASES = [("first", 0, 1, -2), ("a", 0, 1, -1), ("ab", 1, LARGE, 0), ("ab", 3, PAIRS - LARGE - 2, LARGE),
          ("last", 3, 1, PAIRS - 2), ("b", 3, 1, PAIRS - 1)]
LARGE_PHASE, SMALL = 2, 3
BANK_STEPS = ("tok", "xT", "qk", "v", "pv", "back", "proj", "mrow", "fc1", "fc2")
SCORE_STEPS = ("score", "max")


def signals(step, turn):
    x, what, n = step
    if what == "tok":
        return {"tok_made": 1, f"bank_read{turn}": 1}
    if what in ("xT", "v", "back", "proj", "mrow", "fc1", "fc2"):
        s = {f"bank_full{turn}": 1, f"bank_read{turn}": 1}
        if what == "back":
            s["rden_ready"] = 1
        if what == "mrow":
            s["mrow_in"] = 2 * 16
        return s
    if what == "qk":
        return {f"bank_full{turn}": 1, f"bank_read{turn}": 1, "qk_hi_ready": 1}
    if what == "pv":
        return {"pv_done": 1}
    if what == "ot":
        return {f"bank_read{turn}": 1}
    if what in SCORE_STEPS:
        return {f"bank_full{turn}": 1, f"bank_read{turn}": 1}
    if what == "img":
        return {"img_in": 6 * 16}
    if what == "norm":
        s = {"xn_ready": 2}
        if (x, n) == ("b", 0):
            s.update(y_ready=1, hc_ready=1)
        return s
    if what == "split":
        return {"hi_ready": 2, f"split_done_{x}": 2 * 2}
    if what == "sum":
        return {"f_half": 1, "f_ready": 1}
    if what == "stats":
        return {"stats_ready": 2, "var_ready": 1, "rstd_ready": 1} if n % 2 else {}
    if what == "residual":
        return {"hb_ready": 1}
    if what == "const":
        return {"yb_ready": 1}
    if what == "stack":
        return {f"stack_in_{x}": 12 * 16}
    if what == "out":
        return {"out_done": 4 * 16}
    raise KeyError(what)


LEAD = {"out_done": 1}


class Phase:

    def __init__(self, spec, start):
        self.kind, self.branches, self.count, self.first = spec
        self.steps = order(self.kind, self.branches)
        self.start = dict(start)
        self.turn, self.before, self.after = {}, {}, {}
        self.pos = {step: i for i, step in enumerate(self.steps)}
        self.weights = [step for step in self.steps if step[1] == "score"]
        turns, held = list(range(TURNS)), []
        so_far = {}
        for step in self.steps:
            x, what, n = step
            if what == "ot":
                self.turn[step] = self.turn[(x, "pv", 2 * n)]
                held.remove(self.turn[step])
            elif what == "pv" and n % 2 == 1:
                self.turn[step] = self.turn[(x, "pv", n - 1)]
            elif what in BANK_STEPS or what in SCORE_STEPS:
                i = self.pos[step]
                if what in SCORE_STEPS:
                    allowed = range(SCORE_TURNS)
                elif what == "pv" or any(s[1] in SCORE_STEPS for s in self.steps[max(0, i - NEAR):i]):
                    allowed = range(SCORE_TURNS, TURNS)
                else:
                    allowed = range(TURNS)
                self.turn[step] = next(t for t in turns if t in allowed and t not in held)
                turns.remove(self.turn[step])
                turns.append(self.turn[step])
                if what == "pv":
                    held.append(self.turn[step])
            self.before[step] = dict(so_far)
            for name, k in signals(step, self.turn.get(step)).items():
                so_far[name] = so_far.get(name, 0) + k
            self.after[step] = dict(so_far)
        self.per = so_far
        self.end = {k: self.start.get(k, 0) + self.count * so_far.get(k, 0) for k in {**start, **so_far}}

    def value(self, name, inside, it):
        base = self.start.get(name, 0) + inside
        per = self.per.get(name, 0)
        if self.count == 1 or per == 0:
            return base
        assert base > 0, name
        return (it - self.first) * per + base

    def upto(self, name, step, it, k=None):
        inside = self.after[step].get(name, 0) if k is None else self.before[step].get(name, 0) + k
        return self.value(name, inside, it)

    def sooner(self, by, step):
        return by in self.pos and self.pos[by] < self.pos[step]

    def seen(self, name, by, step, it, k=None):
        if self.sooner(by, step):
            return self.upto(name, by, it, k)
        if self.count == 1:
            return self.start.get(name) or None
        inside = self.after[by].get(name, 0) if k is None else self.before[by].get(name, 0) + k
        assert self.start[name] + inside > self.per[name]
        return self.value(name, inside - self.per[name], it)

    def ahead(self, name, step, it):
        v = self.value(name, self.before[step].get(name, 0), it)
        return None if isinstance(v, int) and v == 0 else v


def make_phases():
    phases, start = [], dict(LEAD)
    for spec in PHASES:
        phases.append(Phase(spec, start))
        start = phases[-1].end
    return phases


def passes(width):
    if width == D:
        return [(0, 0, 128, 0), (0, 0, 128, 3), (1, 0, 128, 1), (1, 64, 128, 4), (2, 0, 128, 2)]
    if width > 64:
        return [(0, 0, width, 0), (0, 0, width, 3), (1, 0, 64, 1), (2, 0, width - 64, 2)]
    return [(0, 0, width, 0), (0, 0, width, 3), (1, 0, width, 1)]


def build(nc, I, out):
    f32, f32r = mybir.dt.float32, mybir.dt.float32r
    ALU, ACT, AX = mybir.AluOpType, mybir.ActivationFunctionType, mybir.AxisListType
    phases = make_phases()
    with ExitStack() as ctx:
        def sb(name, shape, dt=f32):
            return ctx.enter_context(nc.sbuf_tensor(name, shape, dt))

        ident = sb("ident", [128, 128])
        ones = sb("ones", [1, 128])
        neg_half = sb("neg_half", [T, 8])
        pos = sb("pos", [T, 2, D])
        w_tok = sb("w_tok", [2 * CH * PS, PS // 2, D])
        w_in = {x: sb(f"w_in_{x}", [128, NPASS, 3 * D], f32r) for x in "ab"}
        w_out = {x: sb(f"w_out_{x}", [128, NPASS, D], f32r) for x in "ab"}
        w_fc1 = sb("w_fc1", [128, NPASS, HID], f32r)
        w_fc2 = sb("w_fc2", [128, HC, sum(KEEP_CH)])
        bias_qk = sb("bias_qk", [128, 3])
        bias_fc1 = sb("bias_fc1", [128, 3, HC])
        const_out = {x: sb(f"const_out_{x}", [T, D]) for x in "ab"}
        const_fc2 = sb("const_fc2", [T, D])
        gain = sb("gain", [128, 3])
        shift = sb("shift", [128, 3])
        v_bias = sb("v_bias", [128, 2])
        gum_row = sb("gum_row", [1, 3])
        gum_col = sb("gum_col", [3, 1])
        gum_all = sb("gum_all", [128, 3])
        fc1_raw = sb("fc1_raw", [128, HC])
        img = sb("img", [2 * CH * PS, IMW])
        xn = {x: sb(f"xn_{x}", [T, 4, D]) for x in "ab"}
        parts = {x: sb(f"parts_{x}", [128, 4 * 2 * D]) for x in "ab"}
        xT = {x: sb(f"xT_{x}", [128, 3, TP], f32r) for x in "ab"}
        qk_hi = {x: sb(f"qk_hi_{x}", [128, 3, TP]) for x in "ab"}
        q_st = {x: sb(f"q_st_{x}", [128, 6, TP], f32r) for x in "ab"}
        k_st = {x: sb(f"k_st_{x}", [128, 6, TP], f32r) for x in "ab"}
        vt = {x: sb(f"vt_{x}", [T, 4, HEADS, 32]) for x in "ab"}
        probs = sb("probs", [T, 4, 2, TP])
        h = sb("h", [T, 4, D])
        h2 = sb("h2", [T, 4, D])
        h2c = sb("h2c", [T, 4, D])
        y = sb("y", [T, 4, D])
        x2 = sb("x2", [T, 4, D])
        hid = sb("hid", [128, HT_SLOTS, TP])
        stats = {x: sb(f"stats_{x}", [T, 4, 6]) for x in "ab"}
        mv = {x: sb(f"mv_{x}", [T, 4, 2]) for x in "ab"}
        ve = {x: sb(f"ve_{x}", [T, 2, 4]) for x in "ab"}
        rstd = {x: sb(f"rstd_{x}", [T, 2, 4]) for x in "ab"}
        rden = {x: sb(f"rden_{x}", [T, 4, HEADS]) for x in "ab"}
        carrier = sb("carrier", [1, 1 + len(LEAD)])
        neg_max = sb("neg_max", [T, 4, HEADS])
        max_rows = sb("max_rows", [HEADS, TP], f32r)
        xs = {x: parts[x][0:T, :].rearrange("p (t n) -> p t n", t=4) for x in "ab"}
        qk_lo = {x: parts[x][:, 0:3 * TP].rearrange("p (c n) -> p c n", c=3) for x in "ab"}
        oT = qk_hi
        stage = hid[:, :, :].rearrange("p s n -> p (s n)")
        stage_2 = qk_hi["b"][:, :, :].rearrange("p s n -> p (s n)")

        rows = hid[0:3, 7, 0:2 * D]
        bout_row = hid[0:1, 6, 0:D]
        b2_row = hid[0:1, 6, D:2 * D]
        one_row = hid[0:1, HT_SLOTS - 1, :]

        psum = ctx.enter_context(nc.psum_tensor("psum", [128, 8, 512], f32))

        def place(t):
            return 2 * t if t < SCORE_TURNS else t + SCORE_TURNS

        names = sorted({n for p in phases for n in p.end})
        sem = {n: ctx.enter_context(nc.semaphore(n)) for n in names}
        vec_chain = ctx.enter_context(nc.semaphore("vec_chain"))
        setup_in = {2: ctx.enter_context(nc.semaphore("setup_in_2")), 1: ctx.enter_context(nc.semaphore("setup_in_1"))}
        setup_sums = ctx.enter_context(nc.semaphore("setup_sums"))
        setup_done = ctx.enter_context(nc.semaphore("setup_done"))
        setup_link = ctx.enter_context(nc.semaphore("setup_link"))

        def at_stage(n):
            return stage_2 if n == D else stage

        def slots(n):
            return at_stage(n)[:, 0:3 * n].rearrange("p (s n) -> p s n", s=3)

        def raw(n, s):
            return at_stage(n)[:, s * n:(s + 1) * n]

        def raw_hi(n):
            return at_stage(n)[64:128, n:2 * n]

        B_TASKS = ["in_b", "out_b", "const_b", "fc1", "fc2"]
        TASKS = {0: ["tok", "in_a", "out_a", "const_a"], 1: [], 2: B_TASKS, 3: B_TASKS, 4: [], 5: []}

        def loads(k, task):
            set_ = "l" if k == LARGE_PHASE else "s"
            if task == "tok":
                return [(w_tok[:, :, :], I["w_tok"]), (pos[:, :, :], I["pos"]), (ident[:, :], I["ident"]),
                        (rows[0:2, 0:D], I["cls_b"]), (rows[0:2, D:D + D], I["tok_rows"][:, 0:D]),
                        (rden["a"][0:2, 0, 0:6], I["tok_rows"][:, D:TI])] + [
                            (k_st["b"][64 * e + 63:64 * e + 64, t, :].bitcast(f32), one_row) for e in range(2) for t in range(6)]
            if task == "in_a":
                return [(slots(3 * D), I["w_in_a"])]
            if task == "in_b":
                return [(slots(3 * D), I["w_in_b"]), (gain[:, :], I[f"n1{set_}_g"]), (shift[:, :], I[f"n1{set_}_b"])]
            if task == "out_a":
                return [(slots(D), I["w_out_a"]), (bout_row[:, :], I["b_out_a"])]
            if task == "out_b":
                more = [(rows[:, 0:D], I["keep_cols"]), (hid[0:3, 5, 0:3 * 128], I["keep_rows"]),
                        (gum_col[:, :], I["gum_col"])] if k == SMALL else []
                return [(slots(D), I["w_out_b"]), (bout_row[:, :], I["b_out_b"]), (b2_row[:, :], I["b_fc2"])] + more
            if task == "fc1":
                return [(slots(HID), I["w_fc1"]), (gain[:, :], I[f"n2{set_}_g"]), (shift[:, :], I[f"n2{set_}_b"]),
                        (fc1_raw[:, :], I["b_fc1"])]
            if task == "fc2":
                return [(stage_2[:, 0:HC * D].rearrange("p (m n) -> p m n", m=HC), I["w_fc2"])] + (
                    [(gum_row[:, :], I["gum_row"])] if k == SMALL else [])
            return []

        def way(task):
            return 2 if task[:3] in ("out", "con", "fc2") else 1

        at_load, at_task, n_load, n_task = {}, {}, {1: 0, 2: 0}, 0
        for k in range(len(PHASES)):
            for task in TASKS[k]:
                n_load[way(task)] += 16 * len(loads(k, task))
                n_task += 1
                at_load[k, task], at_task[k, task] = n_load[way(task)], n_task

        def setup_sync(sp, k):
            for task in TASKS[k]:
                if way(task) == 1 and at_task[k, task] > 1:
                    sp.wait_ge(setup_done, at_task[k, task] - 1)
                for dst, src in loads(k, task):
                    sp.dma_start(dst, src).then_inc(setup_in[way(task)], 16)

        def setup_tensor(pe, k):
            mm = nc.tensor.matmul
            for task in TASKS[k]:
                pe.wait_ge(setup_in[way(task)], at_load[k, task])
                if at_task[k, task] > 1:
                    pe.wait_ge(setup_done, at_task[k, task] - 1)
                last = None
                if task == "tok":
                    pe.wait_ge(setup_link, 1)
                    mm(psum[0:T, 0, 0:D], rows[0:2, D:D + T], rows[0:2, 0:D], start=True, stop=True)
                    last = mm(psum[0:T, 0, D:2 * D], w_fc2[0:2, 0, 0:T], rows[0:2, 0:D], start=True, stop=True)
                if task == "in_b":
                    for c in range(3):
                        mm(psum[:, 1, c:c + 1], raw(576, 0)[:, c * 128:(c + 1) * 128], shift[:, 0:1], start=True, stop=False)
                        mm(psum[:, 1, c:c + 1], raw_hi(576)[:, c * 128:(c + 1) * 128], shift[64:128, 1:2], start=False, stop=True)
                    for c, n in ((0, 128), (1, 64)):
                        at = 2 * D + c * 128
                        mm(psum[128 - n:128, 2, c:c + 1], raw(576, 0)[:, at:at + n], shift[:, 0:1], start=True, stop=False)
                        last = mm(psum[128 - n:128, 2, c:c + 1], raw_hi(576)[:, at:at + n], shift[64:128, 1:2], start=False, stop=True)
                if task == "out_b" and k == SMALL:
                    pe.wait_ge(setup_link, link_at["cols"])
                    for s in range(3):
                        last = mm(psum[:, s, 0:D], hid[0:3, 5, s * 128:(s + 1) * 128], rows[0:3, 0:D], start=True, stop=True)
                if task in ("const_a", "const_b"):
                    last = mm(psum[0:T, 3, 0:D], ones[0:1, 0:T], bout_row[:, :], start=True, stop=task == "const_a")
                    if task == "const_b":
                        mm(psum[0:T, 3, 0:D], vbr(0), raw(D, 0), start=False, stop=False)
                        last = mm(psum[0:T, 3, 0:D], vbr(1), raw_hi(D), start=False, stop=True)
                if task == "fc1":
                    for n in range(phases[k].branches):
                        low = min(KEEP_CH[n], 128)
                        for m in range(HC):
                            at = psum[:, (0, 2, 3)[n], m:m + 1]
                            last = mm(at, stage[0:low, m * 128:(m + 1) * 128], shift[0:low, 0:1], start=True, stop=low < 128)
                            if low == 128:
                                last = mm(at, raw_hi(HID)[:, m * 128:(m + 1) * 128], shift[64:128, 1:2], start=False, stop=True)
                if task == "fc2":
                    last = mm(psum[0:T, 1, 0:D], ones[0:1, 0:T], b2_row[:, :], start=True, stop=True)
                    if k == SMALL:
                        last = mm(psum[:, 0, 0:3], ones[:, :], gum_row[:, :], start=True, stop=True)
                if last is not None:
                    last.then_inc(setup_sums, 1)

        def vbr(c):
            return stage_2[(0, 64)[c]:128, 3 * D + c * T:3 * D + (c + 1) * T]

        HAS_SUMS = {"tok", "in_b", "const_a", "const_b", "fc1", "fc2"}
        at_sums, n_sums = {}, 0
        for k in range(len(PHASES)):
            for task in TASKS[k]:
                n_sums += task in HAS_SUMS or (task == "out_b" and k == SMALL)
                at_sums[k, task] = n_sums
        link_at = {"cols": None}

        def setup_vector(v, k, links):
            def link(ins):
                links[0] += 1
                ins.then_inc(setup_link, 1)
                v.wait_ge(setup_link, links[0])

            def store(w, n):
                link(nc.vector.tensor_copy(w[:, 0:3, :], slots(n)))
                nc.vector.tensor_tensor(w[:, 3, :], raw(n, 0), w[:, 0, :].bitcast(f32), ALU.subtract)
                return nc.vector.tensor_tensor(w[64:128, 4, :], raw_hi(n), w[64:128, 1, :].bitcast(f32), ALU.subtract)

            for task in TASKS[k]:
                v.wait_ge(setup_in[way(task)], at_load[k, task])
                if task == "tok":
                    link(tok_rows(v))
                if task == "out_b" and k == SMALL:
                    link(nc.vector.tensor_scalar(rows[:, 0:D], rows[:, 0:D], gum_col[:, 0:1], None, ALU.mult))
                if task in HAS_SUMS or (task == "out_b" and k == SMALL):
                    v.wait_ge(setup_sums, at_sums[k, task])
                if task == "tok":
                    last = nc.vector.tensor_tensor(pos[:, :, :], psum[0:T, 0, 0:2 * D].rearrange("p (u n) -> p u n", u=2),
                                                   pos[:, :, :], ALU.add)
                if task in ("in_a", "in_b"):
                    if task == "in_b":
                        nc.vector.tensor_scalar(bias_qk[0:64, :], psum[0:64, 1, 0:3], HD ** -0.5, None, ALU.mult)
                        nc.vector.tensor_copy(bias_qk[64:128, :], psum[64:128, 1, 0:3])
                        nc.vector.tensor_copy(v_bias[:, 0:1], psum[:, 2, 0:1])
                        nc.vector.tensor_copy(v_bias[64:128, 1:2], psum[64:128, 2, 1:2])
                        for s in range(3):
                            link(nc.vector.tensor_scalar(raw(576, s), raw(576, s), gain[:, s:s + 1], None, ALU.mult))
                    for s in range(3):
                        q = raw(576, s)[:, 0:2 * D].rearrange("p (c n) -> p c n", c=3)[:, :, 0:64]
                        link(nc.vector.tensor_scalar(q, q, HD ** -0.5, None, ALU.mult))
                    last = store(w_in[task[-1]], 3 * D)
                if task == "out_a":
                    last = store(w_out["a"], D)
                if task == "out_b":
                    if k == SMALL:
                        for s in range(3):
                            link(nc.vector.tensor_tensor(raw(D, s), psum[:, s, 0:D], raw(D, s), ALU.mult))
                        link(nc.vector.tensor_tensor(bout_row[:, :], psum[0:1, 0, 0:D], bout_row[:, :], ALU.mult))
                        link(nc.vector.tensor_tensor(b2_row[:, :], psum[0:1, 0, 0:D], b2_row[:, :], ALU.mult))
                    link(nc.vector.memset(stage_2[:, 3 * D:3 * D + 2 * T], 1.0))
                    for c in range(2):
                        link(nc.vector.tensor_scalar(vbr(c), vbr(c), v_bias[(0, 64)[c]:128, c:c + 1], None, ALU.mult))
                    last = store(w_out["b"], D)
                if task in ("const_a", "const_b"):
                    last = nc.vector.tensor_copy(const_out[task[-1]][:, :], psum[0:T, 3, 0:D])
                if task == "fc1":
                    for n in range(phases[k].branches):
                        nc.vector.tensor_tensor(bias_fc1[:, n, :], psum[:, (0, 2, 3)[n], 0:HC], fc1_raw[:, :], ALU.add)
                    for s in range(3):
                        link(nc.vector.tensor_scalar(raw(HID, s), raw(HID, s), gain[:, s:s + 1], None, ALU.mult))
                    last = store(w_fc1, HID)
                if task == "fc2":
                    src = stage_2[:, 0:HC * D].rearrange("p (m n) -> p m n", m=HC)
                    if k == LARGE_PHASE:
                        nc.vector.tensor_copy(w_fc2[:, :, 0:D], src)
                    else:
                        link(nc.vector.tensor_copy(gum_all[:, :], psum[:, 0, 0:3]))
                        at = 0
                        for n in range(3):
                            nc.vector.tensor_scalar(w_fc2[:, :, at:at + KEEP_CH[n]], src[:, :, 0:KEEP_CH[n]],
                                                    gum_all[:, n:n + 1], None, ALU.mult)
                            at += KEEP_CH[n]
                    last = nc.vector.tensor_copy(const_fc2[:, :], psum[0:T, 1, 0:D])
                last.then_inc(setup_done, 1)

        def tok_rows(v):
            nc.vector.tensor_copy(w_fc2[0:2, 0, 0:D - T], rows[0:2, D + T:2 * D])
            return nc.vector.tensor_copy(w_fc2[0:2, 0, D - T:T], rden["a"][0:2, 0, 0:6])

        def count_links():
            n = 0
            for k in range(len(PHASES)):
                for task in TASKS[k]:
                    if task == "tok":
                        n += 1
                    if task == "out_b" and k == SMALL:
                        link_at["cols"] = n + 1
                        n += 1 + 5
                    if task == "in_a":
                        n += 3 + 1
                    if task == "in_b":
                        n += 3 + 3 + 1
                    if task == "out_a":
                        n += 1
                    if task == "out_b":
                        n += 1 + 2 + 1
                    if task == "fc1":
                        n += 3 + 1
                    if task == "fc2" and k == SMALL:
                        n += 1
        count_links()

        def tile_mm(dst, lhs, rhs, first, last):
            return nc.tensor.matmul(dst, lhs, rhs, start=first, stop=last)

        def by_feature(dst, x, w, col, width, arrive):
            ps = passes(width)
            for j, (c, r0, r1, s) in enumerate(ps):
                arrive(c)
                ins = tile_mm(dst, w[r0:r1, s, col:col + 128], xT[x][r0:r1, c, :], j == 0, j == len(ps) - 1)
            return ins

        def by_token(dst, x, tt, w, col, n, arrive):
            ps = passes(D)
            for j, (c, r0, r1, s) in enumerate(ps):
                arrive(c)
                ins = tile_mm(dst, xT[x][r0:r1, c, tt * T:(tt + 1) * T], w[r0:r1, s, col:col + n], j == 0, j == len(ps) - 1)
            return ins

        def unit(n):
            g, i, hp = n // 4, (n // 2) % 2, n % 2
            return g, i, hp, 2 * g + hp

        def sync_step(sp, ph, step, it):
            x, what, n = step
            if what == "img":
                b = 2 * (it + 2) + n if ph.count == 1 else sp.snap(2 * (it + 2) + n)
                made = ph.ahead("tok_made", step, it)
                if made is not None:
                    sp.wait_ge(sem["tok_made"], made)
                for g in range(2):
                    for c in range(CH):
                        p = (g * CH + c) * PS
                        at = PS - g * (PS // 2)
                        sp.dma_start(img[p:p + PS, at:at + NP * IMG].rearrange("p (py w) -> p py w", w=IMG),
                                     I["x"][b, c].rearrange("(py ph) w -> ph py w", ph=PS)).then_inc(sem["img_in"], 16)
            if what == "out":
                image = [2 * it + i if ph.count == 1 else sp.snap(2 * it + i) for i in range(2)]
                for i in range(2):
                    st = ("b", "fc2", 2 * ph.branches - 2 + i)
                    sp.wait_ge(sem[f"bank_read{ph.turn[st]}"], ph.upto(f"bank_read{ph.turn[st]}", st, it))
                    for u in range(2):
                        sp.dma_start(out[image[i], u * T:u * T + T - u, :], x2[0:T - u, 2 * i + u, :])\
                            .then_inc(sem["out_done"], 16)
            if what == "stack":
                last = (x, "qk", 2)
                sp.wait_ge(sem[f"bank_read{ph.turn[last]}"], ph.upto(f"bank_read{ph.turn[last]}", last, it))
                for side, dst, kinds in ((0, q_st, "hhl"), (1, k_st, "hlh")):
                    for g, kind in enumerate(kinds):
                        src = qk_hi[x] if kind == "h" else qk_lo[x]
                        for b2 in range(2):
                            r = 64 * side + 32 * b2
                            sp.dma_start(dst[x][g:128:4, 3 * b2:3 * b2 + 3, :].bitcast(f32), src[r:r + 32, :, :])\
                                .then_inc(sem[f"stack_in_{x}"], 16)
            if what == "mrow":
                t = ph.turn[step]
                sp.wait_ge(sem[f"bank_read{t}"], ph.upto(f"bank_read{t}", step, it))
                for e in range(2):
                    sp.dma_start(q_st["b"][64 * e + 63:64 * e + 64, :, :].bitcast(f32),
                                 max_rows[6 * e:6 * e + 6, :].bitcast(f32)).then_inc(sem["mrow_in"], 16)

        def tensor_step(pe, ph, step, it):
            x, what, n = step
            t = ph.turn.get(step)

            def bank_free():
                v = ph.ahead(f"bank_read{t}", step, it)
                if v is not None:
                    pe.wait_ge(sem[f"bank_read{t}"], v)

            if what == "tok":
                bank_free()
                u = n % 2
                pe.wait_ge(sem["img_in"], ph.upto("img_in", ("a", "img", n // 2), it))
                for j in range(PS // 2):
                    at = u * (T - 1) * PS + u * PS + j
                    ins = tile_mm(psum[0:T, place(t), 0:D], img[:, at:at + (T - 1) * PS + 1:PS],
                                  w_tok[:, j, :], j == 0, j == PS // 2 - 1)
                ins.then_inc(sem["tok_made"], 1)
            if what == "xT":
                bank_free()
                s = (x, "split", n // 3)
                pe.wait_ge(sem[f"split_done_{x}"], ph.seen(f"split_done_{x}", s, step, it))
                c = n % 3
                for tt in range(4):
                    ins = nc.tensor.transpose(psum[:, place(t), tt * T:(tt + 1) * T], xs[x][:, tt, c * 128:(c + 1) * 128], ident[0:T, 0:T])
                ins.then_inc(sem[f"bank_full{t}"], 1)
            if what in ("qk", "v", "proj", "fc1"):
                bank_free()
                which = {"qk": 0, "v": 0, "proj": 1, "fc1": 2}[what]
                chunks = [0, 1, 2] if n == 0 and what != "v" else []

                def arrive(c):
                    if c in chunks:
                        chunks.remove(c)
                        wait_read(pe, ph, [(x, "xT", 3 * which + c)], it, t)

                if what == "qk":
                    ins = by_feature(psum[:, place(t), 0:TP], x, w_in[x], n * 128, D, arrive)
                if what == "fc1":
                    ins = by_feature(psum[:, place(t), 0:TP], x, w_fc1, n % HC * 128, KEEP_CH[n // HC], arrive)
                if what in ("v", "proj"):
                    w, col = (w_in[x], 2 * D) if what == "v" else (w_out[x], 0)
                    for u in range(2):
                        ins = by_token(psum[0:T, place(t), u * D:(u + 1) * D], x, 2 * n + u, w, col, D, arrive)
                ins.then_inc(sem[f"bank_full{t}"], 1)
            if what in SCORE_STEPS:
                v = ph.ahead(f"bank_read{t}", step, it)
                if v is not None:
                    pe.wait_ge(sem[f"bank_read{t}"], v)
                pe.wait_ge(sem[f"stack_in_{x}"], ph.seen(f"stack_in_{x}", (x, "stack", 0), step, it))
                if what == "score" and x == "b":
                    pe.wait_ge(sem["mrow_in"], ph.upto("mrow_in", ("b", "mrow", 0), it))
                g, i, hp, tile = unit(n)
                rows_ = 64 if what == "score" else 63
                left, right = (k_st, q_st) if what == "score" else (q_st, k_st)
                for u in range(2):
                    for e in range(2):
                        r = slice(64 * e, 64 * e + rows_)
                        ins = tile_mm(psum[0:T, 2 * t + e, u * TI:(u + 1) * TI],
                                      left[x][r, tile, i * TI + u * T:i * TI + (u + 1) * T],
                                      right[x][r, tile, i * TI:(i + 1) * TI], True, True)
                ins.then_inc(sem[f"bank_full{t}"], 1)
            if what == "pv":
                g, i = n // 2, n % 2
                if i == 0:
                    bank_free()
                wait_read(pe, ph, [(x, "score", 2 * n), (x, "score", 2 * n + 1), (x, "v", i)], it, t if i == 0 else None, step)
                for u in range(2):
                    keys = T - u
                    for hp in range(2):
                        for e in range(2):
                            qd = 2 * hp + e
                            ins = tile_mm(psum[32 * qd:32 * qd + 32, place(t), i * TI:(i + 1) * TI],
                                          vt[x][0:keys, 2 * i + u, 4 * g + qd, :],
                                          probs[0:keys, ph.weights.index((x, "score", 2 * n + hp)) % 4, e, u * TI:(u + 1) * TI],
                                          u == 0, u == 1)
                ins.then_inc(sem["pv_done"], 1)
            if what == "back":
                bank_free()
                wait_read(pe, ph, [(x, "ot", 2)], it, t)
                for g in range(3):
                    ins = nc.tensor.transpose(psum[0:T, place(t), g * 128:(g + 1) * 128], oT[x][:, g, n * T:(n + 1) * T], ident[:, :])
                ins.then_inc(sem[f"bank_full{t}"], 1)
            if what == "mrow":
                bank_free()
                wait_read(pe, ph, [("b", "max", 11)], it, t)
                for tt in range(4):
                    ins = nc.tensor.transpose(psum[0:HEADS, place(t), tt * T:(tt + 1) * T], neg_max[:, tt, :], ident[0:T, 0:T])
                ins.then_inc(sem[f"bank_full{t}"], 1)
            if what == "fc2":
                bank_free()
                br, i = n // 2, n % 2
                width, at = KEEP_CH[br], sum(KEEP_CH[:br])
                for u in range(2):
                    tt = 2 * i + u
                    for m in range(HC):
                        if i == 0 and u == 0:
                            wait_read(pe, ph, [("b", "fc1", br * HC + m)], it, t)
                        ins = tile_mm(psum[0:T, place(t), u * D:u * D + width], hid[:, (br * HC + m) % HT_SLOTS, tt * T:(tt + 1) * T],
                                      w_fc2[:, m, at:at + width], m == 0, m == HC - 1)
                ins.then_inc(sem[f"bank_full{t}"], 1)

        def full(eng, ph, step, it):
            t = ph.turn[step]
            eng.wait_ge(sem[f"bank_full{t}"], ph.upto(f"bank_full{t}", step, it))
            return t

        def copier(x, n):
            return nc.vector if n % 3 == 1 and (x, n) != ("a", 4) else nc.scalar

        def scalar_step(act, ph, step, it):
            x, what, n = step
            if (x, what, n) == ("b", "norm", 0):
                wait_read(act, ph, [("a", "proj", i) for i in range(2)], it)
                val = ph.ahead("f_half", step, it)
                if val is not None:
                    act.wait_ge(sem["f_half"], val)
                nc.scalar.activation(h2c[:, :, :], h2[:, :, :], ACT.Identity).then_inc(sem["hc_ready"], 1)
            if what == "split":
                wait_xn(act, ph, step, it, 0)
                if n == 1:
                    act.wait_ge(sem[f"stack_in_{x}"], ph.seen(f"stack_in_{x}", (x, "stack", 0), step, it))
                else:
                    st = (x, "xT", 5 if n == 2 or x == "a" else 8)
                    if st in ph.pos:
                        act.wait_ge(sem[f"bank_full{ph.turn[st]}"], ph.upto(f"bank_full{ph.turn[st]}", st, it))
                for i in range(2):
                    if i:
                        wait_xn(act, ph, step, it, i)
                    tt = slice(2 * i, 2 * i + 2)
                    nc.scalar.activation(xs[x][:, tt, 0:128].bitcast(f32r), xn[x][:, tt, 0:128], ACT.Identity)
                    nc.scalar.activation(xs[x][:, tt, 192:256].bitcast(f32r), xn[x][:, tt, 128:D], ACT.Identity)\
                        .then_inc(sem["hi_ready"], 1)
            if what == "xT" and copier(x, n) is nc.scalar:
                t = full(act, ph, step, it)
                nc.scalar.activation(xT[x][:, n % 3, :], psum[:, place(t), 0:TP], ACT.Identity).then_inc(sem[f"bank_read{t}"], 1)
            if what == "qk":
                t = full(act, ph, step, it)
                bias = bias_qk[:, n:n + 1] if x == "b" else 0.0
                nc.scalar.activation(qk_hi[x][:, n, :].bitcast(f32r), psum[:, place(t), 0:TP], ACT.Identity, bias=bias)\
                    .then_inc(sem["qk_hi_ready"], 1)
            if what == "v":
                t = full(act, ph, step, it)
                nc.scalar.activation(vt[x][:, 2 * n:2 * n + 2, :, 0:HD],
                                     psum[0:T, place(t), 0:2 * D].rearrange("p (u h d) -> p u h d", u=2, h=HEADS),
                                     ACT.Identity).then_inc(sem[f"bank_read{t}"], 1)
            if what == "score":
                t = ph.turn[step]
                act.wait_ge(sem[f"bank_full{t}"], ph.upto(f"bank_full{t}", step, it))
                w = ph.weights.index(step)
                if w >= 4:
                    x4, _, n4 = ph.weights[w - 4]
                    v = ph.upto("pv_done", (x4, "pv", n4 // 2), it)
                else:
                    v = ph.ahead("pv_done", step, it)
                if v is not None:
                    act.wait_ge(sem["pv_done"], v)
                func, bias = (ACT.Square, 1.0) if x == "a" else (ACT.Exp, 0.0)
                nc.scalar.activation(probs[:, w % 4, :, :], psum[0:T, 2 * t:2 * t + 2, 0:TP], func, bias=bias)\
                    .then_inc(sem[f"bank_read{t}"], 1)
            if what == "mrow":
                t = full(act, ph, step, it)
                nc.scalar.activation(max_rows[:, :], psum[0:HEADS, place(t), 0:TP], ACT.Identity).then_inc(sem[f"bank_read{t}"], 1)
            if what == "fc1":
                t = full(act, ph, step, it)
                if n >= HT_SLOTS:
                    for i in range(2):
                        st = ("b", "fc2", 2 * ((n - HT_SLOTS) // HC) + i)
                        if ph.turn[st] != t:
                            act.wait_ge(sem[f"bank_full{ph.turn[st]}"], ph.upto(f"bank_full{ph.turn[st]}", st, it))
                nc.scalar.activation(hid[:, n % HT_SLOTS, :], psum[:, place(t), 0:TP], ACT.Gelu,
                                     bias=bias_fc1[:, n // HC, n % HC:n % HC + 1]).then_inc(sem[f"bank_read{t}"], 1)

        def wait_xn(eng, ph, step, it, i):
            x, _, n = step
            if n == 1:
                wait_read(eng, ph, [(x, "back", 2 * i + 1)], it)
            else:
                eng.wait_ge(sem["xn_ready"], ph.upto("xn_ready", (x, "norm", n // 2), it, i + 1))

        def pool_step(pool, ph, step, it):
            x, what, n = step
            if what == "stats" and n % 2:
                pool.wait_ge(sem["var_ready"], ph.upto("var_ready", step, it))
                first = 0 if (x, n) == ("b", 1) else 1
                nc.gpsimd.tensor_tensor(rstd[x][:, first:2, :], ve[x][:, first:2, :],
                                        neg_half[:, 4 * first:8].rearrange("p (a b) -> p a b", b=4), ALU.pow).then_inc(sem["rstd_ready"], 1)
            if what == "residual":
                pool.wait_ge(sem["xn_ready"], ph.upto("xn_ready", ("a", "norm", 0), it))
                for name in ("y_ready", "hc_ready"):
                    val = ph.ahead(name, step, it)
                    if val is not None:
                        pool.wait_ge(sem[name], val)
                nc.gpsimd.tensor_tensor(h2[:, :, :], h[:, :, :], const_out["a"][:, :].unsqueeze(1).to_broadcast([T, 4, D]),
                                        ALU.add).then_inc(sem["hb_ready"], 1)
            if what == "const":
                pool.wait_ge(sem["y_ready"], ph.seen("y_ready", ("b", "norm", 0), step, it))
                nc.gpsimd.tensor_tensor(y[:, :, :], y[:, :, :], const_out["b"][:, :].unsqueeze(1).to_broadcast([T, 4, D]),
                                        ALU.add).then_inc(sem["yb_ready"], 1)
            if what == "sum":
                pool.wait_ge(sem["xn_ready"], ph.upto("xn_ready", ("b", "norm", 1), it))
                pool.wait_ge(sem["hc_ready"], ph.seen("hc_ready", ("b", "norm", 0), step, it))
                nc.gpsimd.tensor_tensor(x2[:, :, :], x2[:, :, :], h2c[:, :, :], ALU.add).then_inc(sem["f_half"], 1)
                pool.wait_ge(sem["f_half"], ph.upto("f_half", step, it))
                nc.gpsimd.tensor_tensor(x2[:, :, :], x2[:, :, :], const_fc2[:, :].unsqueeze(1).to_broadcast([T, 4, D]),
                                        ALU.add).then_inc(sem["f_ready"], 1)
            if what == "split" and lo_engine(x, n) is nc.gpsimd:
                low_parts(pool, ph, step, it)

        def lo_engine(x, n):
            return nc.vector if x == "b" and n > 0 else nc.gpsimd

        def low_parts(eng, ph, step, it):
            x, _, n = step
            for i in range(2):
                eng.wait_ge(sem["hi_ready"], ph.upto("hi_ready", step, it, i + 1))
                tt = slice(2 * i, 2 * i + 2)
                lo_engine(x, n).tensor_tensor(xs[x][:, tt, 128:192].bitcast(f32r), xn[x][:, tt, 0:64],
                                              xs[x][:, tt, 0:64], ALU.subtract).then_inc(sem[f"split_done_{x}"], 1)
                high = xs[x][:, tt, 64:320].rearrange("p t (a b) -> p t a b", a=2)[:, :, :, 0:64]
                lo_engine(x, n).tensor_tensor(xs[x][:, tt, 256:384].rearrange("p t (a b) -> p t a b", a=2).bitcast(f32r),
                                              xn[x][:, tt, 64:D].rearrange("p t (a b) -> p t a b", a=2), high,
                                              ALU.subtract).then_inc(sem[f"split_done_{x}"], 1)

        def vector_step(v, ph, step, it):
            x, what, n = step
            if what == "tok":
                t = ph.turn[step]
                v.wait_ge(sem["tok_made"], ph.upto("tok_made", step, it))
                val = ph.ahead("hb_ready", step, it)
                if val is not None:
                    v.wait_ge(sem["hb_ready"], val)
                nc.vector.tensor_tensor(h[:, n, :], psum[0:T, place(t), 0:D], pos[:, n % 2, :], ALU.add).then_inc(sem[f"bank_read{t}"], 1)
            if what == "stats":
                norm, i = (x, n // 2), n % 2
                src = {("a", 0): h, ("b", 0): h2, ("b", 1): x2}[norm]
                made = {("a", 0): [("a", "tok", 2 * i), ("a", "tok", 2 * i + 1)], ("b", 0): [("a", "proj", i)],
                        ("b", 1): [("b", "proj", i)]}[norm]
                wait_read(v, ph, made, it)
                for tt in (2 * i, 2 * i + 1):
                    ins = nc.vector.bn_stats(stats[x][:, tt, :], src[:, tt, :])
                if i == 1:
                    ins.then_inc(sem["stats_ready"], 1)
                    v.wait_ge(sem["stats_ready"], ph.upto("stats_ready", step, it, 1))
                    nc.vector.memset(carrier[:, 0:1], 0.0)
                    for tt in range(4):
                        ins = nc.vector.bn_aggr(mv[x][:, tt, :], stats[x][:, tt, :])
                    ins.then_inc(sem["stats_ready"], 1)
                    v.wait_ge(sem["stats_ready"], ph.upto("stats_ready", step, it, 2))
                    var = mv[x][:, :, 1]
                    if norm == ("b", 0):
                        nc.vector.tensor_scalar(ve[x][:, 0, :], var, EPS, None, ALU.add)
                    two = (1.0 + EPS, EPS * EPS) if norm == ("b", 0) else (1.0, EPS)
                    nc.vector.tensor_scalar(ve[x][:, 1, :], var, two[0], two[1], ALU.mult, ALU.add).then_inc(sem["var_ready"], 1)
            if what == "norm":
                src = {("a", 0): h, ("b", 0): h2, ("b", 1): x2}[x, n]
                v.wait_ge(sem["rstd_ready"], ph.upto("rstd_ready", (x, "stats", 2 * n + 1), it))
                read_xn(v, ph, step, it)
                for tt in range(4):
                    ins = nc.vector.tensor_scalar(xn[x][:, tt, :], src[:, tt, :], mv[x][:, tt, 0:1], rstd[x][:, 1, tt:tt + 1],
                                                  ALU.subtract, ALU.mult)
                    if tt % 2:
                        ins.then_inc(sem["xn_ready"], 1)
                if (x, n) == ("b", 0):
                    for tt in range(4):
                        ins = nc.vector.tensor_scalar(y[:, tt, :], src[:, tt, :], mv[x][:, tt, 0:1], rstd[x][:, 0, tt:tt + 1],
                                                      ALU.subtract, ALU.mult)
                    ins.then_inc(sem["y_ready"], 1)
            if what == "split" and lo_engine(x, n) is nc.vector:
                low_parts(v, ph, step, it)
            if what == "xT" and copier(x, n) is nc.vector:
                t = full(v, ph, step, it)
                nc.vector.tensor_copy(xT[x][:, 1, :], psum[:, place(t), 0:TP]).then_inc(sem[f"bank_read{t}"], 1)
            if what == "qk":
                t = ph.turn[step]
                v.wait_ge(sem["qk_hi_ready"], ph.upto("qk_hi_ready", step, it))
                bias = bias_qk[:, n:n + 1] if x == "b" else 0.0
                nc.vector.scalar_tensor_tensor(qk_lo[x][:, n, :].bitcast(f32r), psum[:, place(t), 0:TP], bias, qk_hi[x][:, n, :],
                                               ALU.add, ALU.subtract).then_inc(sem[f"bank_read{t}"], 1)
            if what == "max":
                t = ph.turn[step]
                g, i, hp, tile = unit(n)
                v.wait_ge(sem[f"bank_full{t}"], ph.upto(f"bank_full{t}", step, it))
                dst = neg_max[:, 2 * i:2 * i + 2, :].rearrange("p u (e t) -> p e u t", e=2)[:, :, :, tile]
                src = psum[0:T, 2 * t:2 * t + 2, 0:TP].rearrange("p e (u k) -> p e u k", u=2)[:, :, :, 0:NTOK]
                nc.vector.tensor_reduce(dst, src, AX.X, ALU.max, negate=True).then_inc(sem[f"bank_read{t}"], 1)
            if what == "ot":
                t = ph.turn[step]
                v.wait_ge(sem["pv_done"], ph.upto("pv_done", (x, "pv", 2 * n + 1), it))
                if x == "a":
                    for i in range(2):
                        ins = nc.vector.tensor_scalar(oT[x][:, n, i * TI:(i + 1) * TI], psum[:, place(t), i * TI:(i + 1) * TI],
                                                      psum[:, place(t), (i + 1) * TI - 1:(i + 1) * TI], None, ALU.add)
                else:
                    ins = nc.vector.tensor_copy(oT[x][:, n, :], psum[:, place(t), 0:TP])
                ins.then_inc(sem[f"bank_read{t}"], 1)
            if what == "back":
                t = full(v, ph, step, it)
                if n == 0:
                    read_xn(v, ph, step, it)
                o = psum[0:T, place(t), 0:3 * 128].rearrange("p (h d) -> p h d", h=HEADS)
                nc.vector.reciprocal(rden[x][:, n, :], o[:, :, HD]).then_inc(sem["rden_ready"], 1)
                v.wait_ge(sem["rden_ready"], ph.upto("rden_ready", step, it))
                nc.vector.tensor_tensor(xn[x][:, n, :].rearrange("p (h d) -> p h d", h=HEADS), o[:, :, 0:HD],
                                        rden[x][:, n, :].unsqueeze(2).to_broadcast([T, HEADS, HD]), ALU.mult)\
                    .then_inc(sem[f"bank_read{t}"], 1)
            if what == "proj":
                t = full(v, ph, step, it)
                if x == "a":
                    v.wait_ge(sem["hb_ready"], ph.seen("hb_ready", ("a", "residual", 0), step, it))
                    dst = src = h2
                else:
                    v.wait_ge(sem["yb_ready"], ph.upto("yb_ready", ("b", "const", 0), it))
                    val = ph.ahead("out_done", step, it)
                    if val is not None:
                        v.wait_ge(sem["out_done"], val)
                    dst, src = x2, y
                nc.vector.tensor_tensor(dst[:, 2 * n:2 * n + 2, :], psum[0:T, place(t), 0:2 * D].rearrange("p (u n) -> p u n", u=2),
                                        src[:, 2 * n:2 * n + 2, :], ALU.add).then_inc(sem[f"bank_read{t}"], 1)
            if what == "fc2":
                t = full(v, ph, step, it)
                br, i = n // 2, n % 2
                v.wait_ge(sem["f_ready"], ph.upto("f_ready", ("b", "sum", 0), it))
                if br:
                    wait_read(v, ph, [("b", "fc2", n - 2)], it)
                w = KEEP_CH[br]
                acc = x2[:, 2 * i:2 * i + 2, 0:w]
                nc.vector.tensor_tensor(acc, psum[0:T, place(t), 0:2 * D].rearrange("p (u n) -> p u n", u=2)[:, :, 0:w],
                                        acc, ALU.add).then_inc(sem[f"bank_read{t}"], 1)

        def read_xn(eng, ph, step, it):
            val = ph.ahead(f"split_done_{step[0]}", step, it)
            if val is not None:
                eng.wait_ge(sem[f"split_done_{step[0]}"], val)

        def wait_read(eng, ph, steps, it, free=None, step=None):
            last = {}
            for st in sorted((st for st in steps if st in ph.pos), key=lambda st: (not step or ph.sooner(st, step), ph.pos[st])):
                last[ph.turn[st]] = st
            for t, st in last.items():
                if step and not ph.sooner(st, step):
                    if ph.count > 1 and t != free:
                        eng.wait_ge(sem[f"bank_read{t}"], ph.seen(f"bank_read{t}", st, step, it))
                elif t != free:
                    eng.wait_ge(sem[f"bank_read{t}"], ph.upto(f"bank_read{t}", st, it))

        def run(eng, ph, do):
            if ph.count > 1:
                with eng.Fori(ph.first, ph.first + ph.count) as it:
                    for step in ph.steps:
                        do(eng, ph, step, it)
            else:
                for step in ph.steps:
                    do(eng, ph, step, ph.first)

        links = [0]
        init = ctx.enter_context(nc.semaphore("init"))
        for k, ph in enumerate(phases):
            with nc.Block() as block:
                @block.sync
                def _(sp):
                    if k == 0:
                        sp.wait_ge(init, 10)
                    setup_sync(sp, k)
                    run(sp, ph, sync_step)
                    if k == len(phases) - 1:
                        sp.wait_ge(sem["out_done"], ph.end["out_done"])

                @block.gpsimd
                def _(pool):
                    if k == 0:
                        nc.gpsimd.memset(neg_half[:, :], -0.5).then_inc(init, 1)
                        nc.gpsimd.memset(vt["a"][:, :, :, :], 1.0).then_inc(init, 1)
                        nc.gpsimd.memset(vt["b"][:, :, :, :], 1.0).then_inc(init, 1)
                        nc.gpsimd.memset(img[:, :], 0.0).then_inc(init, 1)
                        for st in (q_st["b"], k_st["b"]):
                            nc.gpsimd.memset(st[:, :, :].bitcast(f32), 0.0).then_inc(init, 1)
                        nc.gpsimd.memset(one_row, 1.0).then_inc(init, 1)
                        pool.wait_ge(init, 10)
                    if TASKS[k]:
                        pool.wait_ge(setup_done, at_task[k, TASKS[k][-1]])
                    run(pool, ph, pool_step)

                @block.vector
                def _(v):
                    if k == 0:
                        nc.vector.memset(ones[:, :], 1.0).then_inc(init, 1)
                        for st in (q_st["a"], k_st["a"]):
                            nc.vector.memset(st[:, :, :].bitcast(f32), 0.0).then_inc(init, 1)
                        for at, (name, lead) in enumerate(LEAD.items()):
                            nc.vector.memset(carrier[:, 1 + at:2 + at], 0.0).then_inc(sem[name], lead)
                    setup_vector(v, k, links)
                    run(v, ph, vector_step)

                @block.scalar
                def _(act):
                    if k == 0:
                        act.wait_ge(init, 10)
                    if TASKS[k]:
                        act.wait_ge(setup_done, at_task[k, TASKS[k][-1]])
                    run(act, ph, scalar_step)

                @block.tensor
                def _(pe):
                    if k == 0:
                        pe.wait_ge(init, 10)
                    setup_tensor(pe, k)
                    if TASKS[k]:
                        pe.wait_ge(setup_done, at_task[k, TASKS[k][-1]])
                    run(pe, ph, tensor_step)


def kernel(**inputs):
    import concourse.bacc as bacc
    from concourse.bass_utils import run_bass_kernel_spmd

    def get(name):
        return np.asarray(inputs[name])

    def stack(w):
        w = w.reshape(D, -1)
        return np.ascontiguousarray(np.stack([w[0:128], np.concatenate([w[0:64], w[128:192]]), w[64:192]], 1))

    cols = [side * D + (2 * (b2 * 3 + c) + e) * HD + d
            for c in range(3) for side in range(2) for b2 in range(2) for e in range(2) for d in range(HD)]
    cols += list(range(2 * D, 3 * D))
    f = np.float32
    pos = np.zeros((TI, D), f)
    pos[:NTOK] = get("L0_tok_pos_embed")
    tok_rows = np.zeros((2, TI), f)
    tok_rows[0, 0] = 1.0
    tok_rows[1, 1:NTOK] = 1.0
    w_tok = get("L0_tok_W").reshape(D, CH, PS, 2, PS // 2).transpose(3, 1, 2, 4, 0).reshape(2 * CH * PS, PS // 2, D)
    keep_rows = np.zeros((3, 3, 128), f)
    row_of = stack(np.arange(D))[:, :, 0].T
    for n in range(3):
        keep_rows[n] = row_of < KEEP_HEADS[n] * HD
    keep_cols = np.array([[c < KEEP_CH[n] for c in range(D)] for n in range(3)], f)
    gum = get("L0_ffn_gumbel_weights")
    arrays = {
        "x": get("x"), "w_tok": w_tok, "pos": pos.reshape(2, T, D).transpose(1, 0, 2), "ident": np.eye(128, dtype=f),
        "cls_b": np.stack([get("L0_tok_class_token")[0], get("L0_tok_b")]), "tok_rows": tok_rows,
        "w_in_a": stack(get("L0_attn_w_qkv")[:, cols]), "w_out_a": stack(get("L0_attn_w_proj")),
        "b_out_a": get("L0_attn_b_proj")[None],
        "w_in_b": stack(get("L0_ffn_w_qkv")[:, cols]), "w_out_b": stack(get("L0_ffn_w_proj")),
        "b_out_b": get("L0_ffn_b_proj")[None],
        "w_fc1": stack(get("L0_ffn_w_fc1")), "b_fc1": get("L0_ffn_b_fc1").reshape(HC, 128).T,
        "w_fc2": get("L0_ffn_w_fc2").reshape(HC, 128, D).transpose(1, 0, 2), "b_fc2": get("L0_ffn_b_fc2")[None],
        "keep_rows": keep_rows.reshape(3, 3 * 128), "keep_cols": keep_cols,
        "gum_col": gum[:, None], "gum_row": gum[None],
    }
    for name in ("n1l", "n1s", "n2l", "n2s"):
        for part in "gb":
            arrays[f"{name}_{part}"] = stack(get(f"L0_ffn_{name}_{part}"))[:, :, 0]
    arrays = {k: np.ascontiguousarray(v) for k, v in arrays.items()}
    nc = bacc.Bacc("TRN2", target_bir_lowering=False, num_devices=1)
    given = {k: nc.dram_tensor(f"in_{k}", v.shape, mybir.dt.from_np(v.dtype), kind="ExternalInput").ap()
             for k, v in arrays.items()}
    out = nc.dram_tensor("out", (B, NTOK, D), mybir.dt.float32, kind="ExternalOutput").ap()
    build(nc, given, out)
    r = run_bass_kernel_spmd(nc, [{f"in_{k}": v for k, v in arrays.items()}], core_ids=[0])
    return r.results[0]["out"]
```
